# Optimizing a Trainium2 kernel written in Bass

```python
import numpy as np
import jax
import jax.numpy as jnp

def _softmax(x, axis=-1):
    return jax.nn.softmax(x, axis=axis)

def _gelu(x):
    return jax.nn.gelu(x, approximate=True)

def _silu(x):
    return jax.nn.silu(x)

def _sigmoid(x):
    return jax.nn.sigmoid(x)

def _layernorm(x, axis=-1, eps=1e-05):
    m = jnp.mean(x, axis=axis, keepdims=True)
    v = jnp.var(x, axis=axis, keepdims=True)
    return (x - m) / jnp.sqrt(v + eps)

def _scatter_add(tgt, idx, src, axis=0):
    return tgt.at[idx].add(src)

def _segment_sum(src, seg, n):
    return jax.ops.segment_sum(src, seg, n)
kernel_name = 'mk_hybrid_d1_jaxref_r8_04bc92'

def setup_inputs(seed: int=0):
    np.random.seed(seed)
    _w = jnp.asarray

    def _L0_attn_a_setup():
        import jax, jax.numpy as jnp
        import numpy as np
        from jax import lax

        def _phi(x):
            return jax.nn.elu(x) + 1.0
        key = jax.random.key(seed)
        ks = jax.random.split(key, 5)
        B, T, D, H = (8, 512, 128, 64)
        x = jax.random.normal(ks[0], (B, T, D), dtype=jnp.float32)
        W_q = jax.random.normal(ks[1], (D, H), dtype=jnp.float32) * (1.0 / np.sqrt(D))
        W_k = jax.random.normal(ks[2], (D, H), dtype=jnp.float32) * (1.0 / np.sqrt(D))
        W_v = jax.random.normal(ks[3], (D, H), dtype=jnp.float32) * (1.0 / np.sqrt(D))
        W_o = jax.random.normal(ks[4], (H, D), dtype=jnp.float32) * (1.0 / np.sqrt(H))
        return {'x': x, 'W_q': W_q, 'W_k': W_k, 'W_v': W_v, 'W_o': W_o}
    _L0_attn_a_in = _L0_attn_a_setup()

    def _L0_attn_b_setup():
        import jax, jax.numpy as jnp
        import numpy as np
        from jax import lax
        B, S, H = (8, 512, 128)
        key = jax.random.key(seed)
        ks = jax.random.split(key, 9)
        x = jax.random.normal(ks[0], (B, S, H), dtype=jnp.float32)
        time_decay = jax.random.normal(ks[1], (H,), dtype=jnp.float32) * 0.01
        time_mix_k = jnp.ones((H,), dtype=jnp.float32) * 0.5
        time_mix_v = jnp.ones((H,), dtype=jnp.float32) * 0.5
        time_mix_r = jnp.ones((H,), dtype=jnp.float32) * 0.5
        sc = 1.0 / np.sqrt(H)
        Wk = jax.random.uniform(ks[2], (H, H), jnp.float32, -sc, sc)
        Wv = jax.random.uniform(ks[3], (H, H), jnp.float32, -sc, sc)
        Wr = jax.random.uniform(ks[4], (H, H), jnp.float32, -sc, sc)
        Wo = jax.random.uniform(ks[5], (H, H), jnp.float32, -sc, sc)
        return {'x': x, 'time_decay': time_decay, 'time_mix_k': time_mix_k, 'time_mix_v': time_mix_v, 'time_mix_r': time_mix_r, 'Wk': Wk, 'Wv': Wv, 'Wr': Wr, 'Wo': Wo}
    _L0_attn_b_in = _L0_attn_b_setup()

    def _L0_ffn_setup():
        import jax, jax.numpy as jnp
        import numpy as np
        D_MODEL = 128
        D_FF = 512
        N_EXPERTS = 8
        INIT_SCALE = 0.1

        def _trunc_normal(key, shape, std):
            return std * jax.random.truncated_normal(key, -2.0, 2.0, shape, dtype=jnp.float32)
        key = jax.random.key(seed)
        ks = jax.random.split(key, 5)
        x = jax.random.normal(ks[0], (4, 128, D_MODEL), dtype=jnp.float32)
        router_W = _trunc_normal(ks[1], (D_MODEL, N_EXPERTS), INIT_SCALE / np.sqrt(D_MODEL))
        router_b = jnp.zeros((N_EXPERTS,), dtype=jnp.float32)
        W1 = _trunc_normal(ks[2], (N_EXPERTS, D_MODEL, D_FF), INIT_SCALE / np.sqrt(D_MODEL))
        b1 = jnp.zeros((N_EXPERTS, D_FF), dtype=jnp.float32)
        W2 = _trunc_normal(ks[3], (N_EXPERTS, D_FF, D_MODEL), INIT_SCALE / np.sqrt(D_FF))
        b2 = jnp.zeros((N_EXPERTS, D_MODEL), dtype=jnp.float32)
        return {'x': x, 'router_W': router_W, 'router_b': router_b, 'W1': W1, 'b1': b1, 'W2': W2, 'b2': b2}
    _L0_ffn_in = _L0_ffn_setup()
    _d = {'L0_attn_a_x': _L0_attn_a_in['x'], 'L0_attn_a_W_q': _L0_attn_a_in['W_q'], 'L0_attn_a_W_k': _L0_attn_a_in['W_k'], 'L0_attn_a_W_v': _L0_attn_a_in['W_v'], 'L0_attn_a_W_o': _L0_attn_a_in['W_o'], 'L0_attn_b_time_decay': _L0_attn_b_in['time_decay'], 'L0_attn_b_time_mix_k': _L0_attn_b_in['time_mix_k'], 'L0_attn_b_time_mix_v': _L0_attn_b_in['time_mix_v'], 'L0_attn_b_time_mix_r': _L0_attn_b_in['time_mix_r'], 'L0_attn_b_Wk': _L0_attn_b_in['Wk'], 'L0_attn_b_Wv': _L0_attn_b_in['Wv'], 'L0_attn_b_Wr': _L0_attn_b_in['Wr'], 'L0_attn_b_Wo': _L0_attn_b_in['Wo'], 'L0_ffn_router_W': _L0_ffn_in['router_W'], 'L0_ffn_router_b': _L0_ffn_in['router_b'], 'L0_ffn_W1': _L0_ffn_in['W1'], 'L0_ffn_b1': _L0_ffn_in['b1'], 'L0_ffn_W2': _L0_ffn_in['W2'], 'L0_ffn_b2': _L0_ffn_in['b2']}
    _x0 = _d['L0_attn_a_x']
    _d['L0_attn_a_x'] = jax.random.normal(jax.random.fold_in(jax.random.key(seed), 1), (4, 1024, 128), dtype=_x0.dtype)
    del _x0
    return _d

def reference(L0_attn_a_x, L0_attn_a_W_q, L0_attn_a_W_k, L0_attn_a_W_v, L0_attn_a_W_o, L0_attn_b_time_decay, L0_attn_b_time_mix_k, L0_attn_b_time_mix_v, L0_attn_b_time_mix_r, L0_attn_b_Wk, L0_attn_b_Wv, L0_attn_b_Wr, L0_attn_b_Wo, L0_ffn_router_W, L0_ffn_router_b, L0_ffn_W1, L0_ffn_b1, L0_ffn_W2, L0_ffn_b2):

    def _L0_attn_a_ref(x, W_q, W_k, W_v, W_o):
        import jax, jax.numpy as jnp
        import numpy as np
        from jax import lax

        def _phi(x):
            return jax.nn.elu(x) + 1.0
        B, T, D = x.shape
        H = W_q.shape[1]
        q = _phi(jnp.einsum('btd,dh->bth', x, W_q))
        k = _phi(jnp.einsum('btd,dh->bth', x, W_k))
        v = jnp.einsum('btd,dh->bth', x, W_v)
        qT = jnp.swapaxes(q, 0, 1)
        kT = jnp.swapaxes(k, 0, 1)
        vT = jnp.swapaxes(v, 0, 1)
        S0 = jnp.zeros((B, H, H), dtype=x.dtype)
        z0 = jnp.zeros((B, H), dtype=x.dtype)

        def step(carry, inp):
            S, z = carry
            q_t, k_t, v_t = inp
            S = S + k_t[:, :, None] * v_t[:, None, :]
            z = z + k_t
            o_t = jnp.einsum('bij,bj->bi', S, q_t)
            denom = jnp.maximum(jnp.sum(z * q_t, axis=-1, keepdims=True), 1e-06)
            return ((S, z), o_t / denom)
        (_, _), oT = lax.scan(step, (S0, z0), (qT, kT, vT))
        o = jnp.swapaxes(oT, 0, 1)
        return jnp.einsum('bth,hd->btd', o, W_o)

    def _L0_attn_b_ref(x, time_decay, time_mix_k, time_mix_v, time_mix_r, Wk, Wv, Wr, Wo):
        import jax, jax.numpy as jnp
        import numpy as np
        from jax import lax
        B, S, H = (8, 512, 128)
        d = jnp.exp(-jnp.exp(time_decay))
        b, s, h = x.shape

        def step(state, xt):
            new_state = xt + state * d
            return (new_state, state)
        init = jnp.zeros((b, h), dtype=x.dtype)
        _, prev = lax.scan(step, init, jnp.swapaxes(x, 0, 1))
        prev = jnp.swapaxes(prev, 0, 1)
        k_in = x * time_mix_k + prev * (1.0 - time_mix_k)
        v_in = x * time_mix_v + prev * (1.0 - time_mix_v)
        r_in = x * time_mix_r + prev * (1.0 - time_mix_r)
        _k = jnp.einsum('bsh,oh->bso', k_in, Wk)
        v = jnp.einsum('bsh,oh->bso', v_in, Wv)
        r = jax.nn.sigmoid(jnp.einsum('bsh,oh->bso', r_in, Wr))
        out = r * jnp.einsum('bsh,oh->bso', v, Wo)
        return out

    def _L0_ffn_ref(x, router_W, router_b, W1, b1, W2, b2):
        import jax, jax.numpy as jnp
        import numpy as np
        D_MODEL = 128
        D_FF = 512
        N_EXPERTS = 8
        INIT_SCALE = 0.1

        def _trunc_normal(key, shape, std):
            return std * jax.random.truncated_normal(key, -2.0, 2.0, shape, dtype=jnp.float32)
        logits = jnp.einsum('bsd,de->bse', x.astype(jnp.float32), router_W) + router_b
        probs = jax.nn.softmax(logits, axis=-1)
        top1 = jnp.argmax(probs, axis=-1)
        mask = jax.nn.one_hot(top1, N_EXPERTS, dtype=x.dtype)
        gates = mask * probs.astype(x.dtype)
        h = jax.nn.relu(jnp.einsum('bsd,edf->besf', x, W1) + b1[:, None, :])
        y = jnp.einsum('besf,efd->besd', h, W2) + b2[:, None, :]
        out = jnp.einsum('bse,besd->bsd', gates, y)
        return out
    x = L0_attn_a_x
    x = x + _L0_attn_a_ref(_layernorm(x, axis=-1), L0_attn_a_W_q, L0_attn_a_W_k, L0_attn_a_W_v, L0_attn_a_W_o)
    x = x + _L0_ffn_ref(_layernorm(x, axis=-1), L0_ffn_router_W, L0_ffn_router_b, L0_ffn_W1, L0_ffn_b1, L0_ffn_W2, L0_ffn_b2)
    x = x + _L0_attn_b_ref(_layernorm(x, axis=-1), L0_attn_b_time_decay, L0_attn_b_time_mix_k, L0_attn_b_time_mix_v, L0_attn_b_time_mix_r, L0_attn_b_Wk, L0_attn_b_Wv, L0_attn_b_Wr, L0_attn_b_Wo)
    x = x + _L0_ffn_ref(_layernorm(x, axis=-1), L0_ffn_router_W, L0_ffn_router_b, L0_ffn_W1, L0_ffn_b1, L0_ffn_W2, L0_ffn_b2)
    return x

_drawn_inputs = setup_inputs


def setup_inputs(seed=0):
    import zlib

    import numpy as np

    out = dict(_drawn_inputs(seed))
    spreads = {'L0_attn_b_time_mix_k': (0.5, 0.2),
     'L0_attn_b_time_mix_v': (0.5, 0.6),
     'L0_attn_b_time_mix_r': (0.5, 0.6),
     'L0_ffn_router_b': (0.0, 0.279),
     'L0_ffn_b1': (0.0, 0.8),
     'L0_ffn_b2': (0.0, 0.276)}
    factors = {'L0_attn_a_W_q': 6.012,
     'L0_attn_a_W_k': 5.62,
     'L0_attn_a_W_v': 3.245,
     'L0_attn_a_W_o': 3.477,
     'L0_attn_b_time_decay': 64.0,
     'L0_ffn_W1': 8.0,
     'L0_ffn_W2': 8.0}
    for name, (base, spread) in spreads.items():
        noise = np.random.default_rng([zlib.crc32(name.encode()), seed]).standard_normal(out[name].shape)
        drawn = base * np.exp(spread * noise) if base else spread * noise
        out[name] = jnp.asarray(drawn.astype(out[name].dtype))
    for name, factor in factors.items():
        out[name] = (out[name] * factor).astype(out[name].dtype)
    return out
```

```python
from contextlib import ExitStack

import concourse.bass as bass
from concourse import mybir

ALU = mybir.AluOpType
ACT = mybir.ActivationFunctionType
F32 = mybir.dt.float32
BF16 = mybir.dt.bfloat16
I32 = mybir.dt.int32
AX_X = mybir.AxisListType.X

P = 128
GT = 4
EPS = 1e-5
ROUND = 12582912.0
NB = 3
ND = 6


def after(eng, sem, n):
    if not isinstance(n, int) or n > 0:
        eng.wait_ge(sem, n)


def hybrid_block(nc, x, w_q, w_k, w_v, w_o, time_decay, mix_v, mix_r, rw_v, rw_r, rw_o,
                 router_w, router_b, w1, b1, w2, b2, out):
    B, T, D = x.shape
    H = w_q.shape[1]
    E, _, DF = w1.shape
    assert D == P and 2 * H == P
    TOK = B * T
    NT = TOK // P
    NG = NT // GT
    GPB = T // P // GT
    assert GPB == 2 and NG == 2 * B
    C = DF // P
    ST = NT + E - 1
    UN = 6
    assert ST % UN >= 2 and UN % ND == 0 and UN % NB == 0
    GW = GT * P
    SPB = 2 * GT - 1
    YC = P + 1

    xt = x.rearrange("b t d -> (b t) d").rearrange("(n p) d -> p n d", p=P)
    ot = out.rearrange("b t d -> (b t) d").rearrange("(n p) d -> p n d", p=P)
    rows_dram = [nc.dram_tensor(f"rows{l}", [TOK, D], F32).ap() for l in range(2)]
    y_dram = [nc.dram_tensor(f"y{l}", [TOK + ST * P, D], F32).ap() for l in range(2)]

    with ExitStack() as ctx:
        def sb(name, shape, dt=F32):
            return ctx.enter_context(nc.sbuf_tensor(name, shape, dt))

        def sem(name):
            return ctx.enter_context(nc.semaphore(name))

        bank = [ctx.enter_context(nc.psum_tensor(f"bank{i}", [P, 512], F32)) for i in range(8)]

        LG_BANK = (3, 6)

        ident = sb("ident", [P, P])
        causal = sb("causal", [P, P])
        before = sb("before", [P, P], BF16)
        ones_bf = sb("ones_bf", [P, P], BF16)
        ones_col = sb("ones_col", [P, 1])
        neg_half = sb("neg_half", [P, GT])
        rev8 = sb("rev8", [P, E])
        iota_p = sb("iota_p", [P, P])
        part1 = sb("part1", [P, 1])
        tile_base = sb("tile_base", [P, NT, ST], BF16)
        spare = sb("spare", [P, ST])
        restart = sb("restart", [P, E, NT])
        wvk = sb("wvk", [P, 2 * H])
        wq = sb("wq", [P, H])
        wox = sb("wox", [P, YC])
        vec = sb("vec", [P, 3])
        mix_c = sb("mix_c", [P, 2])
        edec = sb("edec", [P, 1])
        decay = sb("decay", [P, 1])
        rwv = sb("rwv", [P, P])
        rwr = sb("rwr", [P, P])
        rwo = sb("rwo", [P, P])
        rwoT = sb("rwoT", [P, P])
        wx = sb("wx", [P, 2, P])
        wp = sb("wp", [P, 2, P])
        rtw = sb("rtw", [P, E])
        rtb = sb("rtb", [P, E])
        b1n = sb("b1n", [E * C, P])
        b1T = sb("b1T", [P, E * C])
        b2b = sb("b2b", [P, E, D])
        w2s = sb("w2s", [P, E, C, D])
        xres = sb("xres", [P, NT, D])
        stats = sb("stats", [P, 2, GT, 6])
        mv = sb("mv", [P, 2, GT, 2])
        nmean = sb("nmean", [P, 2, 2, GT])
        veps = sb("veps", [P, 2, 2, GT])
        rstd = sb("rstd", [P, 2, 2, GT])
        xn = [[sb(f"xn{w}{p}", [P, GT, D]) for p in range(2)] for w in range(2)]
        xnT = [sb(f"xnT{p}", [P, GW]) for p in range(2)]
        xn2T = sb("xn2T", [P, GW])
        ex = sb("ex", [P, GW])
        vk = [sb(f"vk{p}", [P, GW]) for p in range(2)]
        qT = [sb(f"qT{p}", [H, GW]) for p in range(2)]
        kv = [sb(f"kv{p}", [P, GT, 2 * H]) for p in range(2)]
        zT = [sb(f"zT{p}", [H, GW]) for p in range(2)]
        op = [sb(f"op{p}", [P, GW]) for p in range(2)]
        am = sb("am", [P, GT, P])
        state = [sb(f"state{c}", [H, H]) for c in range(SPB)]
        rden = sb("rden", [P, 2, GT])
        sc = [sb(f"sc{p}", [P, 1 + GW]) for p in range(2)]
        sg = sb("sg", [P, GT, D])
        tm = sb("tm", [P, GT, D])
        yin = [sb(f"yin{p}", [P, GT, D]) for p in range(2)]
        lg = sb("lg", [P, NT, E])
        mx = sb("mx", [P, NT])
        ld = sb("ld", [P, NT, E])
        le = sb("le", [P, NT, E])
        sm = sb("sm", [P, NT])
        gate = sb("gate", [P, NT])
        rv = sb("rv", [P, NT, E])
        top = sb("top", [P, NT])
        oh = sb("oh", [P, NT, E], BF16)
        tot = sb("tot", [P, E, NT])
        cum = sb("cum", [P, E, NT])
        exc = sb("exc", [P, E, NT])
        etiles = sb("etiles", [P, 3, E])
        ebase = sb("ebase", [P, E])
        slot_e = sb("slot_e", [P, E, NT])
        pos = sb("pos", [P, NT])
        hi = sb("hi", [P, 2, NT])
        lo = sb("lo", [P, NT])
        ecmp = sb("ecmp", [1, ST, E])
        ecnt = sb("ecnt", [1, ST])
        etab = sb("etab", [1, ST + 1], I32)
        lo1h = sb("lo1h", [P, NT, P], BF16)
        hi1h = sb("hi1h", [P, NT, ST], BF16)
        hid = sb("hid", [P, NT, 2, ST], BF16)
        ivh = sb("ivh", [P, ST])
        iv = sb("iv", [P, ST])
        ivz = sb("ivz", [P, ST])
        gidx = sb("gidx", [P, ST], I32)
        sidx = sb("sidx", [P, ST], I32)
        xs = [sb(f"xs{b}", [P, D]) for b in range(ND)]
        xsT = [sb(f"xsT{b}", [P, P]) for b in range(NB)]
        w1s = [sb(f"w1s{b}", [P, DF]) for b in range(ND)]
        hT = [sb(f"hT{b}", [P, C, P]) for b in range(NB)]
        ys = [sb(f"ys{b}", [P, D]) for b in range(ND)]

        s_const = sem("s_const")
        s_memset = sem("s_memset")
        s_settled = sem("s_settled")
        s_zeroed = sem("s_zeroed")
        s_wattn = sem("s_wattn")
        s_wmix = sem("s_wmix")
        s_wffn = sem("s_wffn")
        s_decay = sem("s_decay")
        s_setup_pe = sem("s_setup_pe")
        s_setup_dve = sem("s_setup_dve")
        s_x_in = [sem(f"s_x_in{p}") for p in range(2)]

        NAMES = ("stats aggr ln rstd xn xT xTe x2 x2T x2Te logits lgs st2 ag2 ln2 rs2 xn2 "
                 "vkp qp exp v min phi z zq kvT kv scores am upd state o oe y dmax rden xnew "
                 "col scan mix sig vm")
        AS = {n: sem(f"a_{n}") for n in NAMES.split() if n not in ("x2", "col", "scan", "mix", "sig", "vm")}
        BS = {n: sem(f"b_{n}") for n in ("stats aggr ln rstd xn xT xTe x2 x2T x2Te logits lgs st2 ag2 ln2 rs2 xn2 "
                                         "xnew col scan mix sig vm").split()}
        s_rows = [[sem(f"s_rows{l}{p}") for p in range(2)] for l in range(2)]
        s_yin = [[sem(f"s_yin{l}{p}") for p in range(2)] for l in range(2)]
        s_route = [sem(f"s_route{l}") for l in range(2)]
        s_sub = [sem(f"s_sub{l}") for l in range(2)]
        s_lexp = [sem(f"s_lexp{l}") for l in range(2)]
        s_oh = [sem(f"s_oh{l}") for l in range(2)]
        s_count = [sem(f"s_count{l}") for l in range(2)]
        s_etab = [sem(f"s_etab{l}") for l in range(2)]
        s_onehots = [sem(f"s_onehots{l}") for l in range(2)]
        s_inv = [sem(f"s_inv{l}") for l in range(2)]
        s_idx = [sem(f"s_idx{l}") for l in range(2)]
        s_gat = [[sem(f"s_gat{l}_{b}") for b in range(ND)] for l in range(2)]
        s_w1 = [[sem(f"s_w1{l}_{b}") for b in range(ND)] for l in range(2)]
        s_sct = [[sem(f"s_sct{l}_{b}") for b in range(ND)] for l in range(2)]
        s_xsT = [sem(f"s_xsT{l}") for l in range(2)]
        s_xsTe = [sem(f"s_xsTe{l}") for l in range(2)]
        s_hA = [sem(f"s_hA{l}") for l in range(2)]
        s_hD = [sem(f"s_hD{l}") for l in range(2)]
        s_rA = [sem(f"s_rA{l}") for l in range(2)]
        s_rD = [sem(f"s_rD{l}") for l in range(2)]
        s_ye = [sem(f"s_ye{l}") for l in range(2)]
        s_ys = [sem(f"s_ys{l}") for l in range(2)]
        s_fin = sem("s_fin")
        s_out = [sem(f"s_out{p}") for p in range(2)]

        def settle(eng, n):
            if not isinstance(n, int):
                eng.sem_inc(s_settled, 1)

        def tiles(g, n=GT):
            return bass.ds(g * GT, n)

        def slots(eng, slot):
            for k in range(3):
                slot(k // 2, k % 2)
            with eng.Fori(0, (NG - 4) // 2) as u:
                slot(u + 1, 1)
                slot(u + 2, 0)
            for k in range(NG - 1, NG + 2):
                slot(k // 2, k % 2)

        def live(m, p, back):
            q = (p - back) % 2
            mm = m + (p - back - q) // 2
            return None if isinstance(mm, int) and not 0 <= mm < NG // 2 else (mm, q)

        def slot_tiles(eng, step):
            for i in range(UN):
                step(i, i, 0)
            with eng.Fori(1, ST // UN) as u:
                for r in range(UN):
                    step(UN * u + r, r, u)
            for i in range(ST // UN * UN, ST):
                step(i, i % UN, i // UN)

        def ahead(i, r, n, by):
            if isinstance(i, int) and i + by >= ST:
                return None
            return i + by, (r + by) % UN, n + (r + by) // UN

        block = ctx.enter_context(nc.Block())

        @block.sync
        def _(sp):
            def load_x(m, p):
                after(sp, s_x_in[p], 16 * m)
                sp.dma_start(xres[:, tiles(2 * m + p), :], xt[:, tiles(2 * m + p), :]).then_inc(s_x_in[p], 16)

            load_x(0, 0)
            load_x(0, 1)
            sp.dma_start(rtw[:], router_w).then_inc(s_wffn, 16)
            sp.dma_start(rtb[:], router_b.rearrange("(o e) -> o e", o=1).to_broadcast([P, E])).then_inc(s_wffn, 16)
            sp.dma_start(b1n[:], b1.rearrange("e (c f) -> (e c) f", c=C)).then_inc(s_wffn, 16)
            with sp.Fori(1, NG // 2) as m:
                load_x(m, 0)
                load_x(m, 1)
            sp.dma_start(b2b[:].rearrange("p e d -> p (e d)"),
                         b2.rearrange("e d -> (e d)").rearrange("(o n) -> o n", o=1).to_broadcast([P, E * D])
                         ).then_inc(s_wffn, 16)
            for e in range(E):
                sp.dma_start(w2s[:, e], w2[e].rearrange("(c f) d -> f c d", c=C)).then_inc(s_wffn, 16)

            for l in range(2):
                S = (AS, BS)[l]

                def rows_out(m, p):
                    after(sp, S["xn2"], 2 * m + p + 1)
                    sp.dma_start(rows_dram[l].rearrange("(n p) d -> p n d", p=P)[:, tiles(2 * m + p), :],
                                 xn[1][p][:]).then_inc(s_rows[l][p], 16)

                def load_y(ll, m, p):
                    used = BS["x2"] if ll == 0 else s_fin
                    after(sp, used, 2 * m + p - 1)
                    sp.dma_start(yin[p][:], y_dram[ll][0:TOK, :].rearrange("(n p) d -> p n d", p=P)[
                        :, tiles(2 * m + p), :]).then_inc(s_yin[ll][p], 16)

                if l == 0:
                    with sp.Fori(0, NG // 2) as m:
                        rows_out(m, 0)
                        rows_out(m, 1)
                else:
                    load_y(0, 0, 0)
                    load_y(0, 0, 1)
                    with sp.Fori(1, NG // 2) as m:
                        load_y(0, m, 0)
                        rows_out(m - 1, 0)
                        load_y(0, m, 1)
                        rows_out(m - 1, 1)
                    rows_out(NG // 2 - 1, 0)
                    rows_out(NG // 2 - 1, 1)

                sp.wait_ge(s_etab[l], 1)

                def load_w1(i, r, n):
                    after(sp, s_hD[l], i - ND + 1)
                    e = sp.value_load(etab[0:1, bass.ds(i, 1)], min_val=0, max_val=E - 1)
                    sp.dma_start(w1s[r % ND][:], w1[bass.ds(e, 1)].rearrange("o d f -> (o d) f")
                                 ).then_inc(s_w1[l][r % ND], 16)

                slot_tiles(sp, load_w1)
                for b in range(ND):
                    sp.wait_ge(s_sct[l][b], 16 * len(range(b, ST, ND)))
            load_y(1, 0, 0)
            load_y(1, 0, 1)
            with sp.Fori(1, NG // 2) as m:
                load_y(1, m, 0)
                load_y(1, m, 1)

        @block.gpsimd
        def _(pool):
            nc.gpsimd.memset(ident[:], 0.0)
            nc.gpsimd.memset(causal[:], 1.0)
            nc.gpsimd.memset(before[:], 1.0)
            nc.gpsimd.memset(neg_half[:], -0.5)
            nc.gpsimd.memset(ones_col[:], 1.0)
            nc.gpsimd.memset(ones_bf[:], 1.0).then_inc(s_memset, 1)
            pool.wait_ge(s_memset, 1)
            nc.gpsimd.affine_select(out=ident[:], in_=ident[:], compare_op=ALU.not_equal, fill=1.0, base=0,
                                    pattern=[[-1, P]], channel_multiplier=1)
            nc.gpsimd.affine_select(out=causal[:], in_=causal[:], compare_op=ALU.is_ge, fill=0.0, base=0,
                                    pattern=[[1, P]], channel_multiplier=-1)
            nc.gpsimd.affine_select(out=before[:], in_=before[:], compare_op=ALU.is_gt, fill=0.0, base=0,
                                    pattern=[[1, P]], channel_multiplier=-1).then_inc(s_const, 1)

            def norm(S, w, names, m, p, read, stored=None):
                ln, rs, done = names
                g = 2 * m + p
                pool.wait_ge(S[ln], g + 1)
                nc.gpsimd.tensor_tensor(rstd[:, w, p], veps[:, w, p], neg_half[:], ALU.pow).then_inc(S[rs], 1)
                pool.wait_ge(S[rs], g + 1)
                after(pool, S[read], g - 1)
                if stored is not None:
                    after(pool, stored[p], 16 * m)
                for j in range(GT):
                    last = nc.gpsimd.tensor_scalar(xn[w][p][:, j], xres[:, g * GT + j], nmean[:, w, p, j:j + 1],
                                                   rstd[:, w, p, j:j + 1], ALU.add, ALU.mult)
                last.then_inc(S[done], 1)

            for l in range(2):
                S = (AS, BS)[l]
                norm(S, 0, ("ln", "rstd", "xn"), 0, 0, "xT")
                for k in range(NG + 1):
                    nxt, prev = live(k // 2, k % 2, -1), live(k // 2, k % 2, 1)
                    if l == 0 and k < NG:
                        pool.wait_ge(AS["exp"], k + 1)
                        nc.gpsimd.tensor_scalar(ex[:], ex[:], 1.0, 0.0, ALU.min, ALU.max).then_inc(AS["min"], 1)
                    if nxt:
                        norm(S, 0, ("ln", "rstd", "xn"), *nxt, "xT")
                    if prev:
                        norm(S, 1, ("ln2", "rs2", "xn2"), *prev, "x2T", s_rows[l])
                if l == 0:
                    nc.gpsimd.iota(rev8[:], pattern=[[-1, E]], base=E, channel_multiplier=0,
                                   allow_small_or_imprecise_dtypes=True)
                    nc.gpsimd.iota(iota_p[:], pattern=[[1, P]], base=0, channel_multiplier=0,
                                   allow_small_or_imprecise_dtypes=True)
                    nc.gpsimd.iota(part1[:], pattern=[[0, 1]], base=1, channel_multiplier=1,
                                   allow_small_or_imprecise_dtypes=True)
                    nc.gpsimd.iota(tile_base[:], pattern=[[P, NT], [0, ST]], base=0, channel_multiplier=0,
                                   allow_small_or_imprecise_dtypes=True)
                    nc.gpsimd.iota(spare[:], pattern=[[P, ST]], base=TOK + 1, channel_multiplier=1,
                                   allow_small_or_imprecise_dtypes=True)
                    nc.gpsimd.memset(restart[:], 1.0).then_inc(s_memset, 1)
                    pool.wait_ge(s_memset, 2)
                    nc.gpsimd.memset(restart[:, :, 0:1], 0.0).then_inc(s_const, 1)

                for p in range(2):
                    pool.wait_ge(s_rows[l][p], 16 * (NG // 2))
                pool.wait_ge(s_idx[l], 1)

                def gather(i):
                    after(pool, s_xsT[l], i - ND + 1)
                    pool.indirect_dma_start(xs[i % ND][:], None, rows_dram[l],
                                            bass.IndirectOffsetOnAxis(ap=gidx[:, i:i + 1], axis=0)
                                            ).then_inc(s_gat[l][i % ND], 16)

                def scatter(i):
                    pool.wait_ge(s_ys[l], i + 1)
                    pool.indirect_dma_start(y_dram[l], bass.IndirectOffsetOnAxis(ap=sidx[:, i:i + 1], axis=0),
                                            ys[i % ND][:], None).then_inc(s_sct[l][i % ND], 16)

                for i in range(ND):
                    gather(i)
                for i in range(ST):
                    scatter(i)
                    if i + ND < ST:
                        gather(i + ND)

        @block.scalar
        def _(act):
            act.dma_start(wvk[:, 0:H], w_v).then_inc(s_wattn, 16)
            act.dma_start(wvk[:, H:2 * H], w_k).then_inc(s_wattn, 16)
            act.dma_start(wq[:], w_q).then_inc(s_wattn, 16)
            act.wait_ge(s_zeroed, 1)
            act.dma_start(wox[0:H, 0:D], w_o).then_inc(s_wattn, 16)
            act.dma_start(rwv[:], rw_v).then_inc(s_wmix, 16)
            act.dma_start(rwr[:], rw_r).then_inc(s_wmix, 16)
            act.dma_start(rwo[:], rw_o).then_inc(s_wmix, 16)
            for i, v in enumerate((time_decay, mix_v, mix_r)):
                act.dma_start(vec[:, i:i + 1], v.rearrange("(h o) -> h o", o=1)).then_inc(s_wmix, 16)

            def evac_xT(S, m, p, dst, read):
                act.wait_ge(S["xT"], 2 * m + p + 1)
                after(act, *read)
                nc.scalar.copy(dst[:], bank[0][:]).then_inc(S["xTe"], 1)

            def evac_x2T(S, m, p):
                g = 2 * m + p
                act.wait_ge(S["x2T"], g + 1)
                after(act, S["logits"], g)
                nc.scalar.copy(xn2T[:], bank[0][:]).then_inc(S["x2Te"], 1)

            def attn_slot(m, p):
                k = 2 * m + p
                if live(m, p, 0):
                    evac_xT(AS, m, p, xnT[0], (AS["qp"], k))
                    act.wait_ge(AS["vkp"], k + 1)
                    after(act, AS["phi"], k)
                    nc.scalar.activation(ex[H:P, :], bank[1][H:P, :], ACT.Exp)
                    act.wait_ge(AS["qp"], k + 1)
                    nc.scalar.activation(ex[0:H, :], bank[2][0:H, :], ACT.Exp).then_inc(AS["exp"], 1)
                    after(act, AS["o"], k - 1)
                    nc.scalar.copy(vk[p][0:H, :], bank[1][0:H, :]).then_inc(AS["v"], 1)
                if live(m, p, 1):
                    mm, q = live(m, p, 1)
                    act.wait_ge(AS["o"], k)
                    after(act, AS["y"], k - 2)
                    nc.scalar.copy(op[q][0:H, :], bank[5][0:H, :]).then_inc(AS["oe"], 1)
                if live(m, p, 2):
                    evac_x2T(AS, *live(m, p, 2))
                if live(m, p, 0):
                    act.wait_ge(AS["kvT"], k + 1)
                    nc.scalar.copy(kv[p][:], bank[3][:].rearrange("p (j c) -> p j c", j=GT)).then_inc(AS["kv"], 1)

            def mix_slot(m, p):
                k = 2 * m + p
                if live(m, p, 0):
                    evac_xT(BS, m, p, xnT[p], (BS["mix"], k - 1))
                if live(m, p, 2):
                    evac_x2T(BS, *live(m, p, 2))
                if live(m, p, 0):
                    act.wait_ge(BS["mix"], k + 1)
                    after(act, BS["vm"], k)
                    for i in range(2):
                        src = bank[(1, 4)[p] + i][:].rearrange("t (j w d) -> t j w d", j=2, w=2)[:, :, 1]
                        last = nc.scalar.activation(sg[:, 2 * i:2 * i + 2], src, ACT.Sigmoid)
                    last.then_inc(BS["sig"], 1)

            act.wait_ge(s_wmix, 16 * 6)
            nc.scalar.activation(edec[:], vec[:, 0:1], ACT.Exp).then_inc(s_decay, 1)
            act.wait_ge(s_decay, 1)
            nc.scalar.activation(decay[:], edec[:], ACT.Exp, scale=-1.0).then_inc(s_decay, 1)

            for l in range(2):
                slots(act, (attn_slot, mix_slot)[l])
                act.wait_ge(s_sub[l], 1)
                nc.scalar.activation(le[:], ld[:], ACT.Exp).then_inc(s_lexp[l], 1)

                act.wait_ge(s_etab[l], 1)

                def evac_xs(i, r, n):
                    act.wait_ge(s_xsT[l], i + 1)
                    after(act, s_hD[l], i - NB + 1)
                    nc.scalar.copy(xsT[r % NB][:], bank[r % 2][:, 0:P]).then_inc(s_xsTe[l], 1)

                def relu(i, r, n):
                    e = act.value_load(etab[0:1, bass.ds(i, 1)], min_val=0, max_val=E - 1)
                    act.wait_ge(s_hA[l], i + 1)
                    after(act, s_ye[l], i - NB + 1)
                    for c in range(C // 2):
                        last = nc.scalar.activation(hT[r % NB][:, c], bank[2 + r % 2][:, c * P:(c + 1) * P], ACT.Relu,
                                                    bias=b1T[:, bass.ds(e * C + c, 1)])
                    last.then_inc(s_rA[l], 1)

                def step(*at):
                    if ahead(*at, 2):
                        evac_xs(*ahead(*at, 2))
                    if ahead(*at, 1):
                        relu(*ahead(*at, 1))

                evac_xs(0, 0, 0)
                evac_xs(1, 1, 0)
                relu(0, 0, 0)
                slot_tiles(act, step)

            def store(m, p):
                act.wait_ge(s_fin, 2 * m + p + 1)
                act.dma_start(ot[:, tiles(2 * m + p), :], xres[:, tiles(2 * m + p), :]).then_inc(s_out[p], 16)

            with act.Fori(0, NG // 2) as m:
                store(m, 0)
                store(m, 1)
            for p in range(2):
                act.wait_ge(s_out[p], 16 * (NG // 2))

        @block.vector
        def _(dve):
            def tile_of(g, j):
                return xres[:, bass.ds(g * GT + j, 1), :].rearrange("p o d -> p (o d)")

            def moments(S, w, names, m, p, normed):
                st, ag, ln = names
                g = 2 * m + p
                settle(dve, g)
                for j in range(GT):
                    last = nc.vector.bn_stats(stats[:, w, j], tile_of(g, j))
                last.then_inc(S[st], 1)
                dve.wait_ge(S[st], g + 1)
                settle(dve, g)
                for j in range(GT):
                    last = nc.vector.bn_aggr(mv[:, w, j], stats[:, w, j])
                last.then_inc(S[ag], 1)
                dve.wait_ge(S[ag], g + 1)
                after(dve, S[normed], g - 1)
                nc.vector.tensor_scalar(nmean[:, w, p], mv[:, w, :, 0], -1.0, None, ALU.mult)
                nc.vector.tensor_scalar(veps[:, w, p], mv[:, w, :, 1], EPS, None, ALU.add).then_inc(S[ln], 1)

            def first_moments(m, p):
                dve.wait_ge(s_x_in[p], 16 * (m + 1))
                moments(AS, 0, ("stats", "aggr", "ln"), m, p, "xn")

            def logits_out(S, m, p):
                g = 2 * m + p
                dve.wait_ge(S["logits"], g + 1)
                nc.vector.tensor_tensor(lg[:, tiles(g), :],
                                        bank[LG_BANK[S is BS]][:, 0:GT * E].rearrange("p (j e) -> p j e", j=GT),
                                        rtb[:].unsqueeze(1).to_broadcast([P, GT, E]), ALU.add).then_inc(S["lgs"], 1)

            def attn_slot(m, p):
                k = 2 * m + p
                back = live(m, p, 1)
                if back:
                    mm, q = back
                    dve.wait_ge(AS["scores"], k)
                    after(dve, AS["o"], k - 1)
                    nc.vector.tensor_tensor(am[:], bank[4][:].rearrange("p (j t) -> p j t", j=GT),
                                            causal[:].unsqueeze(1).to_broadcast([P, GT, P]), ALU.mult
                                            ).then_inc(AS["am"], 1)
                    dve.wait_ge(AS["upd"], k)
                    after(dve, AS["o"], 2 * mm)
                    for j in range(GT if q == 0 else GT - 1):
                        c = GT * q + j
                        n = SPB * mm + c
                        upd = bank[5][H:P, H * j:H * (j + 1)]
                        if c == 0:
                            nc.vector.tensor_copy(state[c][:], upd).then_inc(AS["state"], 1)
                        else:
                            dve.wait_ge(AS["state"], n)
                            nc.vector.tensor_tensor(state[c][:], upd, state[c - 1][:], ALU.add
                                                    ).then_inc(AS["state"], 1)
                nxt = live(m, p, -1)
                if nxt:
                    first_moments(*nxt)
                if live(m, p, 0):
                    dve.wait_ge(AS["min"], k + 1)
                    after(dve, AS["o"], k - 1)
                    nc.vector.scalar_tensor_tensor(out=vk[p][H:P, :], in0=bank[1][H:P, :], scalar=0.0,
                                                   in1=ex[H:P, :], op0=ALU.max, op1=ALU.add)
                    nc.vector.scalar_tensor_tensor(out=qT[p][:], in0=bank[2][0:H, :], scalar=0.0,
                                                   in1=ex[0:H, :], op0=ALU.max, op1=ALU.add).then_inc(AS["phi"], 1)
                    dve.wait_ge(AS["phi"], k + 1)
                    after(dve, AS["z"], k)
                    nc.vector.tensor_tensor_scan(zT[p][:], ones_col[H:P, 0:1].to_broadcast([H, GW]), vk[p][H:P, :],
                                                 0.0 if p == 0 else zT[0][:, GW - 1:GW], ALU.mult, ALU.add
                                                 ).then_inc(AS["z"], 1)
                    dve.wait_ge(AS["z"], k + 1)
                    after(dve, AS["y"], k - 1)
                    nc.vector.tensor_tensor(op[p][H:P, :], zT[p][:], qT[p][:], ALU.mult).then_inc(AS["zq"], 1)
                if back:
                    dve.wait_ge(AS["y"], k)
                    outs = [bank[6 + i][:, 0:2 * YC].rearrange("p (j c) -> p j c", j=2) for i in range(2)]
                    for i in range(2):
                        last = nc.vector.tensor_scalar(rden[:, 0, 2 * i:2 * i + 2], outs[i][:, :, D], 1e-6, None,
                                                       ALU.max)
                    last.then_inc(AS["dmax"], 1)
                    dve.wait_ge(AS["dmax"], k)
                    nc.vector.reciprocal(rden[:, 1], rden[:, 0]).then_inc(AS["rden"], 1)
                    dve.wait_ge(AS["rden"], k)
                    for j in range(GT):
                        t = tile_of(k - 1, j)
                        last = nc.vector.scalar_tensor_tensor(out=t, in0=outs[j // 2][:, j % 2, 0:D],
                                                              scalar=rden[:, 1, j:j + 1], in1=t,
                                                              op0=ALU.mult, op1=ALU.add)
                    last.then_inc(AS["xnew"], 1)
                    dve.wait_ge(AS["xnew"], k)
                    moments(AS, 1, ("st2", "ag2", "ln2"), mm, q, "xn2")
                if live(m, p, 2):
                    logits_out(AS, *live(m, p, 2))

            def add_y(m, p, sem_in, done, *reads):
                g = 2 * m + p
                dve.wait_ge(sem_in[p], 16 * (m + 1))
                for j in range(GT):
                    t = tile_of(g, j)
                    last = nc.vector.scalar_tensor_tensor(out=t, in0=yin[p][:, j], scalar=gate[:, bass.ds(g * GT + j, 1)],
                                                          in1=t, op0=ALU.mult, op1=ALU.add)
                last.then_inc(done, 1)

            def mix_front(m, p):
                add_y(m, p, s_yin[0], BS["x2"])
                dve.wait_ge(BS["x2"], 2 * m + p + 1)
                moments(BS, 0, ("stats", "aggr", "ln"), m, p, "xn")

            def mix_slot(m, p):
                k = 2 * m + p
                if live(m, p, -1):
                    mix_front(*live(m, p, -1))
                if live(m, p, 0):
                    dve.wait_ge(BS["xTe"], k + 1)
                    after(dve, BS["mix"], k - 1)
                    after(dve, BS["scan"], k)
                    if p == 1:
                        nc.vector.tensor_copy(sc[1][:, 0:1], sc[0][:, GW:GW + 1])
                    nc.vector.tensor_tensor_scan(sc[p][:, 1:1 + GW], decay[:, 0:1].to_broadcast([P, GW]), xnT[p][:],
                                                 0.0 if p == 0 else sc[0][:, GW:GW + 1], ALU.mult, ALU.add
                                                 ).then_inc(BS["scan"], 1)
                back = live(m, p, 1)
                if back:
                    mm, q = back
                    dve.wait_ge(BS["sig"], k)
                    after(dve, BS["xnew"], k - 1)
                    for i in range(2):
                        val = bank[(1, 4)[q] + i][:].rearrange("t (j w d) -> t j w d", j=2, w=2)[:, :, 0]
                        last = nc.vector.tensor_tensor(tm[:, 2 * i:2 * i + 2], sg[:, 2 * i:2 * i + 2], val, ALU.mult)
                    last.then_inc(BS["vm"], 1)
                    dve.wait_ge(BS["vm"], k)
                    nc.vector.tensor_tensor(xres[:, tiles(k - 1), :], xres[:, tiles(k - 1), :], tm[:], ALU.add
                                            ).then_inc(BS["xnew"], 1)
                    dve.wait_ge(BS["xnew"], k)
                    moments(BS, 1, ("st2", "ag2", "ln2"), mm, q, "xn2")
                if live(m, p, 2):
                    logits_out(BS, *live(m, p, 2))

            def route(l):
                n = [0]

                def step(ins):
                    n[0] += 1
                    ins.then_inc(s_route[l], 1)
                    dve.wait_ge(s_route[l], n[0])

                def per_tile(a, k=E):
                    return a.unsqueeze(2).to_broadcast([P, NT, k])

                dve.wait_ge((AS, BS)[l]["lgs"], NG)
                dve.wait_ge(s_const, 2)
                step(nc.vector.tensor_reduce(mx[:], lg[:], AX_X, ALU.max))
                nc.vector.tensor_tensor(ld[:], lg[:], per_tile(mx[:]), ALU.subtract).then_inc(s_sub[l], 1)
                dve.wait_ge(s_sub[l], 1)
                step(nc.vector.scalar_tensor_tensor(out=rv[:], in0=ld[:], scalar=0.0,
                                                    in1=rev8[:].unsqueeze(1).to_broadcast([P, NT, E]),
                                                    op0=ALU.is_equal, op1=ALU.mult))
                step(nc.vector.tensor_reduce(top[:], rv[:], AX_X, ALU.max))
                nc.vector.tensor_tensor(oh[:], rev8[:].unsqueeze(1).to_broadcast([P, NT, E]), per_tile(top[:]),
                                        ALU.is_equal).then_inc(s_oh[l], 1)
                dve.wait_ge(s_lexp[l], 1)
                step(nc.vector.tensor_reduce(sm[:], le[:], AX_X, ALU.add))
                nc.vector.reciprocal(gate[:], sm[:])
                dve.wait_ge(s_count[l], 1)
                step(nc.vector.tensor_copy(tot[:], bank[2][:, 0:NT * E].rearrange("p (t e) -> p e t", e=E)))
                step(nc.vector.tensor_tensor_scan(cum[:].rearrange("p e t -> p (e t)"),
                                                  restart[:].rearrange("p e t -> p (e t)"),
                                                  tot[:].rearrange("p e t -> p (e t)"), 0.0, ALU.mult, ALU.add))
                nc.vector.tensor_tensor(exc[:], cum[:], tot[:], ALU.subtract)
                step(nc.vector.tensor_scalar(etiles[:, 0], cum[:, :, NT - 1], 1.0 / P, (P - 1) / 2 / P, ALU.mult, ALU.add))
                step(nc.vector.tensor_scalar(etiles[:, 1], etiles[:, 0], ROUND, -ROUND, ALU.add, ALU.add))
                step(nc.vector.tensor_tensor_scan(etiles[:, 2], ones_col[:, 0:1].to_broadcast([P, E]), etiles[:, 1],
                                                  0.0, ALU.mult, ALU.add))
                step(nc.vector.tensor_tensor(ebase[:], etiles[:, 2], etiles[:, 1], ALU.subtract))
                step(nc.vector.tensor_tensor(ecmp[:], iota_p[0:1, 0:ST].unsqueeze(2).to_broadcast([1, ST, E]),
                                             etiles[0:1, 2].unsqueeze(1).to_broadcast([1, ST, E]), ALU.is_ge))
                step(nc.vector.tensor_reduce(ecnt[:], ecmp[:], AX_X, ALU.add))
                nc.vector.tensor_scalar(etab[0:1, 0:ST], ecnt[:], float(E - 1), None, ALU.min).then_inc(s_etab[l], 1)
                step(nc.vector.scalar_tensor_tensor(out=slot_e[:], in0=ebase[:].unsqueeze(2).to_broadcast([P, E, NT]),
                                                    scalar=float(P), in1=exc[:], op0=ALU.mult, op1=ALU.add))
                step(nc.vector.tensor_tensor(tot[:], bank[1][:, 0:NT * E].rearrange("p (t e) -> p e t", e=E), slot_e[:],
                                             ALU.add))
                step(nc.vector.tensor_tensor(cum[:], tot[:], oh[:].rearrange("p t e -> p e t"), ALU.mult))
                step(nc.vector.tensor_reduce(pos[:], cum[:].rearrange("p e t -> p t e"), AX_X, ALU.add))
                step(nc.vector.tensor_scalar(hi[:, 0], pos[:], 1.0 / P, -(P - 1) / 2 / P, ALU.mult, ALU.add))
                step(nc.vector.tensor_scalar(hi[:, 1], hi[:, 0], ROUND, -ROUND, ALU.add, ALU.add))
                step(nc.vector.scalar_tensor_tensor(out=lo[:], in0=hi[:, 1], scalar=-float(P), in1=pos[:],
                                                    op0=ALU.mult, op1=ALU.add))
                step(nc.vector.tensor_tensor(hi1h[:], iota_p[:, 0:ST].unsqueeze(1).to_broadcast([P, NT, ST]),
                                             per_tile(hi[:, 1], ST), ALU.is_equal))
                nc.vector.tensor_scalar(hid[:, :, 0], hi1h[:], part1[:, 0:1], None, ALU.mult)
                nc.vector.tensor_tensor(hid[:, :, 1], hi1h[:], tile_base[:], ALU.mult).then_inc(s_onehots[l], 1)
                for q in range(4):
                    t = slice(NT // 4 * q, NT // 4 * (q + 1))
                    nc.vector.tensor_tensor(lo1h[:, t], iota_p[:].unsqueeze(1).to_broadcast([P, NT // 4, P]),
                                            lo[:, t].unsqueeze(2).to_broadcast([P, NT // 4, P]), ALU.is_equal
                                            ).then_inc(s_onehots[l], 1)
                dve.wait_ge(s_inv[l], 1)
                step(nc.vector.tensor_copy(ivh[:], bank[4][:, 0:ST]))
                step(nc.vector.tensor_tensor(iv[:], bank[4][:, ST:2 * ST], ivh[:], ALU.add))
                nc.vector.tensor_scalar(gidx[:], iv[:], -1.0, 0.0, ALU.add, ALU.max)
                step(nc.vector.scalar_tensor_tensor(out=ivz[:], in0=iv[:], scalar=0.0, in1=spare[:],
                                                    op0=ALU.is_equal, op1=ALU.mult))
                nc.vector.scalar_tensor_tensor(out=sidx[:], in0=iv[:], scalar=-1.0, in1=ivz[:],
                                               op0=ALU.add, op1=ALU.add).then_inc(s_idx[l], 1)

            def experts(l):
                def expert(i):
                    return dve.value_load(etab[0:1, bass.ds(i, 1)], min_val=0, max_val=E - 1)

                def relu(i, r, n):
                    e = expert(i)
                    dve.wait_ge(s_hD[l], i + 1)
                    after(dve, s_ye[l], i - NB + 1)
                    for c in range(C // 2, C):
                        last = nc.vector.tensor_scalar(hT[r % NB][:, c], bank[4 + r % 2][:, (c - C // 2) * P:(c - C // 2 + 1) * P],
                                                       b1T[:, bass.ds(e * C + c, 1)], 0.0, ALU.add, ALU.max)
                    last.then_inc(s_rD[l], 1)

                def bias2(i, r, n):
                    b = r % ND
                    e = expert(i)
                    dve.wait_ge(s_ye[l], i + 1)
                    after(dve, s_sct[l][b], 16 * n)
                    nc.vector.tensor_tensor(ys[b][:], bank[6 + r % 2][:, 0:P],
                                            b2b[:, bass.ds(e, 1), :].rearrange("p o d -> p (o d)"), ALU.add
                                            ).then_inc(s_ys[l], 1)

                def step(*at):
                    if ahead(*at, 1):
                        relu(*ahead(*at, 1))
                    bias2(*at)

                dve.wait_ge(s_etab[l], 1)
                relu(0, 0, 0)
                slot_tiles(dve, step)

            nc.vector.memset(wox[:], 0.0).then_inc(s_zeroed, 1)
            dve.wait_ge(s_zeroed, 1)
            nc.vector.memset(wox[H:P, D:YC], 1.0).then_inc(s_zeroed, 1)
            nc.vector.memset(sc[0][:, 0:1], 0.0)
            first_moments(0, 0)

            dve.wait_ge(s_setup_pe, 1)
            nc.vector.tensor_copy(rwoT[:], bank[3][:, 0:P]).then_inc(s_setup_dve, 1)
            nc.vector.tensor_scalar(mix_c[:], vec[:, 1:3], -1.0, 1.0, ALU.mult, ALU.add).then_inc(s_setup_dve, 1)
            dve.wait_ge(s_setup_pe, 2)
            dve.wait_ge(s_setup_dve, 2)
            for w in range(2):
                src = bank[5 - w][:, 0:P]
                nc.vector.tensor_scalar(wx[:, w], src, vec[:, 1 + w:2 + w], None, ALU.mult)
                nc.vector.tensor_scalar(wp[:, w], src, mix_c[:, w:w + 1], None, ALU.mult)
            nc.vector.tensor_copy(b1T[:], bank[4][:, P:P + E * C]).then_inc(s_setup_dve, 1)

            slots(dve, attn_slot)
            route(0)
            experts(0)
            mix_front(0, 0)
            slots(dve, mix_slot)
            route(1)
            experts(1)

            add_y(0, 0, s_yin[1], s_fin)
            add_y(0, 1, s_yin[1], s_fin)
            with dve.Fori(1, NG // 2) as m:
                add_y(m, 0, s_yin[1], s_fin)
                add_y(m, 1, s_yin[1], s_fin)

        @block.tensor
        def _(pe):
            def transpose_x(S, m, p):
                g = 2 * m + p
                pe.wait_ge(S["xn"], g + 1)
                after(pe, S["x2Te"], g - 2)
                for j in range(GT):
                    last = nc.tensor.transpose(bank[0][:, j * P:(j + 1) * P], xn[0][p][:, j], ident[:])
                last.then_inc(S["xT"], 1)

            def transpose_x2(S, m, p):
                g = 2 * m + p
                pe.wait_ge(S["xn2"], g + 1)
                pe.wait_ge(S["xTe"], min(g + 3, NG) if isinstance(g, int) else g + 3)
                for j in range(GT):
                    last = nc.tensor.transpose(bank[0][:, j * P:(j + 1) * P], xn[1][p][:, j], ident[:])
                last.then_inc(S["x2T"], 1)

            def logits(S, m, p):
                g = 2 * m + p
                pe.wait_ge(S["x2Te"], g + 1)
                after(pe, S["lgs"], g)
                if S is AS:
                    pe.wait_ge(S["kv"], min(g + 3, NG) if isinstance(g, int) else g + 3)
                for j in range(GT):
                    last = nc.tensor.matmul(bank[LG_BANK[S is BS]][:, E * j:E * (j + 1)], xn2T[:, j * P:(j + 1) * P],
                                            rtw[:], start=True, stop=True)
                last.then_inc(S["logits"], 1)

            def attn_slot(m, p):
                k = 2 * m + p
                cur, back, old = live(m, p, 0), live(m, p, 1), live(m, p, 2)
                if cur:
                    transpose_x(AS, m, p)
                if back:
                    mm, q = back
                    after(pe, AS["am"], k - 1)
                    for j in range(GT):
                        t = slice(j * P, (j + 1) * P)
                        last = nc.tensor.matmul(bank[4][:, t], vk[q][0:H, t], qT[q][:, t], start=True, stop=True)
                    last.then_inc(AS["scores"], 1)
                    pe.wait_ge(AS["kv"], k)
                    after(pe, AS["state"], SPB * mm + GT * q)
                    settle(pe, k)
                    for j in range(GT if q == 0 else GT - 1):
                        last = nc.tensor.matmul(bank[5][H:P, H * j:H * (j + 1)], kv[q][:, j, 0:H],
                                                kv[q][:, j, H:2 * H], start=True, stop=True)
                    last.then_inc(AS["upd"], 1)
                if cur:
                    pe.wait_ge(AS["xTe"], k + 1)
                    after(pe, AS["phi"], k)
                    after(pe, AS["v"], k)
                    nc.tensor.matmul(bank[1][:], wvk[:], xnT[0][:], start=True, stop=True).then_inc(AS["vkp"], 1)
                    nc.tensor.matmul(bank[2][0:H, :], wq[:], xnT[0][:], start=True, stop=True).then_inc(AS["qp"], 1)
                if back:
                    pe.wait_ge(AS["am"], k)
                    after(pe, AS["oe"], k - 1)
                    for j in range(GT):
                        t = slice(j * P, (j + 1) * P)
                        c = GT * q + j
                        last = nc.tensor.matmul(bank[5][0:H, t], kv[q][:, j, H:2 * H], am[:, j], start=True, stop=(c == 0))
                        if c > 0:
                            pe.wait_ge(AS["state"], SPB * mm + c)
                            settle(pe, mm)
                            last = nc.tensor.matmul(bank[5][0:H, t], state[c - 1][:], qT[q][:, t],
                                                    start=False, stop=True)
                    last.then_inc(AS["o"], 1)
                if old:
                    transpose_x2(AS, *old)
                if cur:
                    pe.wait_ge(AS["phi"], k + 1)
                    pe.wait_ge(AS["v"], k + 1)
                    after(pe, AS["kv"], k)
                    after(pe, AS["lgs"], k - 2)
                    for j in range(GT):
                        last = nc.tensor.transpose(bank[3][:, j * P:(j + 1) * P], vk[p][:, j * P:(j + 1) * P],
                                                   ident[:])
                    last.then_inc(AS["kvT"], 1)
                if back:
                    pe.wait_ge(AS["oe"], k)
                    pe.wait_ge(AS["zq"], k)
                    for j in range(GT):
                        last = nc.tensor.matmul(bank[6 + j // 2][:, YC * (j % 2):YC * (j % 2 + 1)],
                                                op[q][:, j * P:(j + 1) * P], wox[:], start=True, stop=True)
                    last.then_inc(AS["y"], 1)
                if old:
                    logits(AS, *old)

            def mix_slot(m, p):
                k = 2 * m + p
                cur, old = live(m, p, 0), live(m, p, 2)
                if cur:
                    transpose_x(BS, m, p)
                if old:
                    transpose_x2(BS, *old)
                    logits(BS, *old)
                if cur:
                    pe.wait_ge(BS["scan"], k + 1)
                    pe.wait_ge(BS["xTe"], k + 1)
                    after(pe, BS["vm"], k - 1)
                    for j in range(GT):
                        t = slice(j * P, (j + 1) * P)
                        o = bank[(1, 4)[p] + j // 2][:, 2 * P * (j % 2):2 * P * (j % 2 + 1)]
                        nc.tensor.matmul(o, xnT[p][:, t], wx[:].rearrange("p w d -> p (w d)"), start=True, stop=False)
                        last = nc.tensor.matmul(o, sc[p][:, t], wp[:].rearrange("p w d -> p (w d)"),
                                                start=False, stop=True)
                    last.then_inc(BS["mix"], 1)

            def route(l):
                pe.wait_ge(s_oh[l], 1)
                ohf = oh[:].rearrange("p t e -> p (t e)")
                nc.tensor.matmul(bank[1][:, 0:NT * E], before[:], ohf, start=True, stop=True)
                nc.tensor.matmul(bank[2][:, 0:NT * E], ones_bf[:], ohf, start=True, stop=True).then_inc(s_count[l], 1)
                for t in range(NT):
                    if t % (NT // 4) == 0:
                        pe.wait_ge(s_onehots[l], 2 + t // (NT // 4))
                    last = nc.tensor.matmul(bank[4][:, 0:2 * ST], lo1h[:, t], hid[:, t].rearrange("p w s -> p (w s)"),
                                            start=(t == 0), stop=(t == NT - 1))
                last.then_inc(s_inv[l], 1)

            def experts(l):
                def turn(i, r, n):
                    pe.wait_ge(s_gat[l][r % ND], 16 * (n + 1))
                    after(pe, s_xsTe[l], i - 1)
                    nc.tensor.transpose(bank[r % 2][:, 0:P], xs[r % ND][:], ident[:]).then_inc(s_xsT[l], 1)

                def first(i, r, n):
                    pe.wait_ge(s_xsTe[l], i + 1)
                    pe.wait_ge(s_w1[l][r % ND], 16 * (n + 1))
                    for half, ready, used in ((0, s_hA[l], s_rA[l]), (1, s_hD[l], s_rD[l])):
                        after(pe, used, i - 1)
                        for c in range(C // 2):
                            f = (half * (C // 2) + c) * P
                            mm = nc.tensor.matmul(bank[2 + 2 * half + r % 2][:, c * P:(c + 1) * P],
                                                  w1s[r % ND][:, f:f + P], xsT[r % NB][:], start=True, stop=True)
                        mm.then_inc(ready, 1)

                def second(i, r, n):
                    e = pe.value_load(etab[0:1, bass.ds(i, 1)], min_val=0, max_val=E - 1)
                    pe.wait_ge(s_rA[l], i + 1)
                    pe.wait_ge(s_rD[l], i + 1)
                    after(pe, s_ys[l], i - 1)
                    for c in range(C):
                        mm = nc.tensor.matmul(bank[6 + r % 2][:, 0:P], hT[r % NB][:, c],
                                              w2s[:, bass.ds(e, 1), c, :].rearrange("p o d -> p (o d)"),
                                              start=(c == 0), stop=(c == C - 1))
                    mm.then_inc(s_ye[l], 1)

                def step(*at):
                    if ahead(*at, 2):
                        turn(*ahead(*at, 2))
                    if ahead(*at, 1):
                        first(*ahead(*at, 1))
                    second(*at)

                pe.wait_ge(s_etab[l], 1)
                turn(0, 0, 0)
                turn(1, 1, 0)
                first(0, 0, 0)
                slot_tiles(pe, step)

            pe.wait_ge(s_const, 1)
            pe.wait_ge(s_wmix, 16 * 6)
            nc.tensor.transpose(bank[3][:, 0:P], rwo[:], ident[:]).then_inc(s_setup_pe, 1)
            nc.tensor.transpose(bank[4][:, 0:P], rwr[:], ident[:])
            pe.wait_ge(s_wffn, 16 * (4 + E))
            nc.tensor.transpose(bank[4][:, P:P + E * C], b1n[:], ident[0:E * C, 0:E * C])
            pe.wait_ge(s_setup_dve, 1)
            nc.tensor.matmul(bank[5][:, 0:P], rwv[:], rwoT[:], start=True, stop=True).then_inc(s_setup_pe, 1)
            pe.wait_ge(s_setup_dve, 3)
            pe.wait_ge(s_wattn, 64)
            pe.wait_ge(s_zeroed, 2)

            slots(pe, attn_slot)
            route(0)
            experts(0)
            slots(pe, mix_slot)
            route(1)
            experts(1)


_INS = ['L0_attn_a_x', 'L0_attn_a_W_q', 'L0_attn_a_W_k', 'L0_attn_a_W_v', 'L0_attn_a_W_o',
        'L0_attn_b_time_decay', 'L0_attn_b_time_mix_v', 'L0_attn_b_time_mix_r',
        'L0_attn_b_Wv', 'L0_attn_b_Wr', 'L0_attn_b_Wo',
        'L0_ffn_router_W', 'L0_ffn_router_b', 'L0_ffn_W1', 'L0_ffn_b1', 'L0_ffn_W2', 'L0_ffn_b2']


def kernel(**inputs):
    import numpy as _np
    import concourse.bacc as _bacc
    from concourse import mybir as _mybir
    from concourse.bass_utils import run_bass_kernel_spmd as _run

    nc = _bacc.Bacc("TRN2", target_bir_lowering=False, num_devices=1)
    arrays, args = {}, []
    for name in _INS:
        a = _np.ascontiguousarray(inputs[name])
        arrays[f"in_{name}"] = a
        args.append(nc.dram_tensor(f"in_{name}", a.shape, _mybir.dt.from_np(a.dtype), kind="ExternalInput").ap())
    out = nc.dram_tensor("out", inputs['L0_attn_a_x'].shape, _mybir.dt.float32, kind="ExternalOutput").ap()
    hybrid_block(nc, *args, out)
    r = _run(nc, [arrays], core_ids=[0])
    return r.results[0]["out"]
```

```python
from contextlib import ExitStack

import concourse.bass as bass
from concourse import mybir

ALU = mybir.AluOpType
ACT = mybir.ActivationFunctionType
F32 = mybir.dt.float32
BF16 = mybir.dt.bfloat16
I32 = mybir.dt.int32
AX_X = mybir.AxisListType.X

P = 128
GT = 4
EPS = 1e-5
ROUND = 12582912.0
NB = 3
ND = 6


def after(eng, sem, n):
    if not isinstance(n, int) or n > 0:
        eng.wait_ge(sem, n)


def hybrid_block(nc, x, w_q, w_k, w_v, w_o, time_decay, mix_v, mix_r, rw_v, rw_r, rw_o,
                 router_w, router_b, w1, b1, w2, b2, out):
    B, T, D = x.shape
    H = w_q.shape[1]
    NA = (2, 3)
    E, _, DF = w1.shape
    assert D == P and 2 * H == P
    TOK = B * T
    NT = TOK // P
    NG = NT // GT
    GPB = T // P // GT
    assert GPB == 2 and NG == 2 * B
    C = DF // P
    ST = NT + E - 1
    UN = 6
    assert ST % UN >= 2 and UN % ND == 0 and UN % NB == 0
    GW = GT * P
    YC = P + 1

    xt = x.rearrange("b t d -> (b t) d").rearrange("(n p) d -> p n d", p=P)
    rows_dram = [nc.dram_tensor(f"rows{l}", [TOK, 2 * D], F32).ap() for l in range(2)]
    x_mid = nc.dram_tensor("x_mid", [TOK, D], F32).ap()
    x_new = [x_mid, out.rearrange("b t d -> (b t) d")]

    with ExitStack() as ctx:
        def sb(name, shape, dt=F32):
            return ctx.enter_context(nc.sbuf_tensor(name, shape, dt))

        def sem(name):
            return ctx.enter_context(nc.semaphore(name))

        bank = [ctx.enter_context(nc.psum_tensor(f"bank{i}", [P, 512], F32)) for i in range(8)]

        LG_BANK = (3, 6)
        X2_BANK = (0, 3)

        ident = sb("ident", [P, P])
        causal = sb("causal", [P, P])
        before = sb("before", [P, P], BF16)
        ones_bf = sb("ones_bf", [P, P], BF16)
        ones_col = sb("ones_col", [P, 1])
        neg_half = sb("neg_half", [P, GT])
        rev8 = sb("rev8", [P, E])
        iota_p = sb("iota_p", [P, P])
        part1 = sb("part1", [P, 1])
        tile_base = sb("tile_base", [P, NT, ST], BF16)
        spare = sb("spare", [P, ST])
        restart = sb("restart", [P, E, NT])
        wvk = sb("wvk", [P, 2 * H])
        wq = sb("wq", [P, H])
        wox = sb("wox", [P, YC])
        vec = sb("vec", [P, 3])
        mix_c = sb("mix_c", [P, 2])
        edec = sb("edec", [P, 1])
        decay = sb("decay", [P, 1])
        rwv = sb("rwv", [P, P])
        rwr = sb("rwr", [P, P])
        rwo = sb("rwo", [P, P])
        rwoT = sb("rwoT", [P, P])
        wx = sb("wx", [P, 2, P])
        wp = sb("wp", [P, 2, P])
        rtw = sb("rtw", [P, E])
        rtb = sb("rtb", [P, E])
        b1n = sb("b1n", [E * C, P])
        b1T = sb("b1T", [P, E * C])
        b2b = sb("b2b", [P, E, D])
        w2s = sb("w2s", [P, E, C, D])
        xres = sb("xres", [P, NT, D])
        stats = sb("stats", [P, 2, GT, 6])
        mv = sb("mv", [P, 2, 2, GT, 2])
        nmean = sb("nmean", [P, 2, 2, GT])
        veps = sb("veps", [P, 2, 2, GT])
        rstd = sb("rstd", [P, 2, 2, GT])
        nmr = sb("nmr", [P, 2, 2, GT])
        xn = [[sb(f"xn{w}{p}", [P, GT, D]) for p in range(2)] for w in range(2)]
        xnT = [sb(f"xnT{p}", [P, GW]) for p in range(2)]
        xn2T = sb("xn2T", [P, GW])
        ex = sb("ex", [P, GW])
        rl = sb("rl", [P, GW])
        vk = [sb(f"vk{p}", [P, GW]) for p in range(2)]
        qT = [sb(f"qT{p}", [H, GW]) for p in range(2)]
        kv = [sb(f"kv{p}", [P, GT, 2 * H]) for p in range(2)]
        zT = [sb(f"zT{p}", [H, GW]) for p in range(2)]
        op = [sb(f"op{p}", [P, GW]) for p in range(2)]
        am = sb("am", [P, GT, P])
        state = [sb(f"state{p}", [H, GT, H]) for p in range(2)]
        rden = sb("rden", [P, 2, GT])
        sc = [sb(f"sc{p}", [P, 1 + GW]) for p in range(2)]
        sg = sb("sg", [P, GT, D])
        tm = sb("tm", [P, GT, D])
        lg = sb("lg", [P, NT, E])
        mx = sb("mx", [P, NT])
        ld = sb("ld", [P, NT, E])
        le = sb("le", [P, NT, E])
        sm = sb("sm", [P, NT])
        gate = sb("gate", [P, NT])
        rv = sb("rv", [P, NT, E])
        top = sb("top", [P, NT])
        oh = sb("oh", [P, NT, E], BF16)
        tot = sb("tot", [P, E, NT])
        cum = sb("cum", [P, E, NT])
        exc = sb("exc", [P, E, NT])
        etiles = sb("etiles", [P, 3, E])
        ebase = sb("ebase", [P, E])
        slot_e = sb("slot_e", [P, E, NT])
        pos = sb("pos", [P, NT])
        hi = sb("hi", [P, 2, NT])
        lo = sb("lo", [P, NT])
        ecmp = sb("ecmp", [1, ST, E])
        ecnt = sb("ecnt", [1, ST])
        etab = sb("etab", [1, ST + 1], I32)
        lo1h = sb("lo1h", [P, NT, P], BF16)
        hi1h = sb("hi1h", [P, NT, ST], BF16)
        hid = sb("hid", [P, NT, 2, ST], BF16)
        ivh = sb("ivh", [P, ST])
        iv = sb("iv", [P, ST])
        ivz = sb("ivz", [P, ST])
        gidx = sb("gidx", [P, ST], I32)
        sidx = sb("sidx", [P, ST], I32)
        gpart = sb("gpart", [P, 3, NT], BF16)
        grest = sb("grest", [P, 2, NT])
        hig = sb("hig", [P, NT, 3, ST], BF16)
        gsum = sb("gsum", [P, 2, ST])
        gslot = sb("gslot", [P, ST])
        xs = [sb(f"xs{b}", [P, 2 * D]) for b in range(ND)]
        xsT = [sb(f"xsT{b}", [P, P]) for b in range(NB)]
        w1s = [sb(f"w1s{b}", [P, DF]) for b in range(ND)]
        hT = [sb(f"hT{b}", [P, C, P]) for b in range(NB)]
        ys = [sb(f"ys{b}", [P, D]) for b in range(ND)]

        s_const = sem("s_const")
        s_memset = sem("s_memset")
        s_settled = sem("s_settled")
        s_zeroed = sem("s_zeroed")
        s_wattn = sem("s_wattn")
        s_wmix = sem("s_wmix")
        s_router = sem("s_router")
        s_b1 = sem("s_b1")
        s_w2 = sem("s_w2")
        s_decay = sem("s_decay")
        s_setup_pe = sem("s_setup_pe")
        s_setup_dve = sem("s_setup_dve")
        s_x_in = [[sem(f"s_x_in{l}{p}") for p in range(2)] for l in range(2)]

        NORM = "stats rstd xn xnp xT xTe x2T x2Te logits lgs st2 rs2 xn2 xn2p xnew "
        AS = {n: sem(f"a_{n}") for n in (NORM + "vkp qp relk relq v phik phi z zq kvT kv scores am upd "
                                         "state o oe y dmax rden").split()}
        BS = {n: sem(f"b_{n}") for n in (NORM + "scan mix sig vm").split()}
        s_rows = [[sem(f"s_rows{l}{p}") for p in range(2)] for l in range(2)]
        s_xrows = [sem(f"s_xrows{l}") for l in range(2)]
        s_route = [sem(f"s_route{l}") for l in range(2)]
        s_lexp = [sem(f"s_lexp{l}") for l in range(2)]
        s_oh = [sem(f"s_oh{l}") for l in range(2)]
        s_count = [sem(f"s_count{l}") for l in range(2)]
        s_etab = [sem(f"s_etab{l}") for l in range(2)]
        s_onehots = [sem(f"s_onehots{l}") for l in range(2)]
        s_inv = [sem(f"s_inv{l}") for l in range(2)]
        s_idx = [sem(f"s_idx{l}") for l in range(2)]
        s_gates = [sem(f"s_gates{l}") for l in range(2)]
        s_gat = [[sem(f"s_gat{l}_{b}") for b in range(ND)] for l in range(2)]
        s_w1 = [[sem(f"s_w1{l}_{b}") for b in range(ND)] for l in range(2)]
        s_sct = [[sem(f"s_sct{l}_{b}") for b in range(ND)] for l in range(2)]
        s_xsT = [sem(f"s_xsT{l}") for l in range(2)]
        s_xsTe = [sem(f"s_xsTe{l}") for l in range(2)]
        s_hA = [sem(f"s_hA{l}") for l in range(2)]
        s_hD = [sem(f"s_hD{l}") for l in range(2)]
        s_rA = [sem(f"s_rA{l}") for l in range(2)]
        s_rD = [sem(f"s_rD{l}") for l in range(2)]
        s_ye = [sem(f"s_ye{l}") for l in range(2)]
        s_pre = [sem(f"s_pre{l}") for l in range(2)]
        s_ys = [sem(f"s_ys{l}") for l in range(2)]

        def settle(eng, n):
            if not isinstance(n, int):
                eng.sem_inc(s_settled, 1)

        def tiles(g, n=GT):
            return bass.ds(g * GT, n)

        def slots(eng, slot):
            for k in range(3):
                slot(k // 2, k % 2)
            with eng.Fori(0, (NG - 4) // 2) as u:
                slot(u + 1, 1)
                slot(u + 2, 0)
            for k in range(NG - 1, NG + 2):
                slot(k // 2, k % 2)

        def live(m, p, back):
            q = (p - back) % 2
            mm = m + (p - back - q) // 2
            return None if isinstance(mm, int) and not 0 <= mm < NG // 2 else (mm, q)

        def slot_tiles(eng, step):
            for i in range(UN):
                step(i, i, 0)
            with eng.Fori(1, ST // UN) as u:
                for r in range(UN):
                    step(UN * u + r, r, u)
            for i in range(ST // UN * UN, ST):
                step(i, i % UN, i // UN)

        def ahead(i, r, n, by):
            if isinstance(i, int) and i + by >= ST:
                return None
            return i + by, (r + by) % UN, n + (r + by) // UN

        block = ctx.enter_context(nc.Block())

        @block.sync
        def _(sp):
            def load_x(l, m, p):
                after(sp, s_x_in[l][p], 16 * m)
                src = (xt, x_mid.rearrange("(n p) d -> p n d", p=P))[l]
                sp.dma_start(xres[:, tiles(2 * m + p), :], src[:, tiles(2 * m + p), :]).then_inc(s_x_in[l][p], 16)

            for l in range(2):
                S = (AS, BS)[l]
                load_x(l, 0, 0)
                load_x(l, 0, 1)
                if l == 0:
                    sp.dma_start(rtw[:], router_w).then_inc(s_router, 16)
                    sp.dma_start(rtb[:], router_b.rearrange("(o e) -> o e", o=1).to_broadcast([P, E])
                                 ).then_inc(s_router, 16)
                with sp.Fori(1, NG // 2) as m:
                    load_x(l, m, 0)
                    load_x(l, m, 1)
                if l == 0:
                    for dst, src in ((rwv, rw_v), (rwr, rw_r), (rwo, rw_o)):
                        sp.dma_start(dst[:], src).then_inc(s_wmix, 16)
                    for i, v in enumerate((time_decay, mix_v, mix_r)):
                        sp.dma_start(vec[:, i:i + 1], v.rearrange("(h o) -> h o", o=1)).then_inc(s_wmix, 16)
                    sp.dma_start(b1n[:], b1.rearrange("e (c f) -> (e c) f", c=C)).then_inc(s_b1, 16)
                    sp.dma_start(b2b[:].rearrange("p e d -> p (e d)"),
                                 b2.rearrange("e d -> (e d)").rearrange("(o n) -> o n", o=1).to_broadcast([P, E * D])
                                 ).then_inc(s_w2, 16)
                    for e in range(E):
                        sp.dma_start(w2s[:, e], w2[e].rearrange("(c f) d -> f c d", c=C)).then_inc(s_w2, 16)

                rows = rows_dram[l].rearrange("(n p) (w d) -> p n w d", p=P, w=2)

                def rows_out(m, p):
                    g = 2 * m + p
                    sp.wait_ge(S["xnew"], g + 1)
                    settle(sp, g)
                    sp.dma_start(rows[:, tiles(g), 1, :], xres[:, tiles(g), :]).then_inc(s_xrows[l], 16)
                    sp.wait_ge(S["xn2"], g + 1)
                    sp.wait_ge(S["xn2p"], g + 1)
                    settle(sp, g)
                    sp.dma_start(rows[:, tiles(g), 0, :], xn[1][p][:]).then_inc(s_rows[l][p], 16)

                with sp.Fori(0, NG // 2) as m:
                    rows_out(m, 0)
                    rows_out(m, 1)

                sp.wait_ge(s_etab[l], 1)

                def load_w1(i, r, n):
                    after(sp, s_hD[l], i - ND + 1)
                    e = sp.value_load(etab[0:1, bass.ds(i, 1)], min_val=0, max_val=E - 1)
                    sp.dma_start(w1s[r % ND][:], w1[bass.ds(e, 1)].rearrange("o d f -> (o d) f")
                                 ).then_inc(s_w1[l][r % ND], 16)

                slot_tiles(sp, load_w1)
                for b in range(ND):
                    sp.wait_ge(s_sct[l][b], 16 * len(range(b, ST, ND)))

        @block.gpsimd
        def _(pool):
            nc.gpsimd.memset(ident[:], 0.0)
            nc.gpsimd.memset(causal[:], 1.0)
            nc.gpsimd.memset(before[:], 1.0)
            nc.gpsimd.memset(neg_half[:], -0.5)
            nc.gpsimd.memset(ones_col[:], 1.0)
            nc.gpsimd.memset(ones_bf[:], 1.0).then_inc(s_memset, 1)
            pool.wait_ge(s_memset, 1)
            nc.gpsimd.affine_select(out=ident[:], in_=ident[:], compare_op=ALU.not_equal, fill=1.0, base=0,
                                    pattern=[[-1, P]], channel_multiplier=1)
            nc.gpsimd.affine_select(out=causal[:], in_=causal[:], compare_op=ALU.is_ge, fill=0.0, base=0,
                                    pattern=[[1, P]], channel_multiplier=-1)
            nc.gpsimd.affine_select(out=before[:], in_=before[:], compare_op=ALU.is_gt, fill=0.0, base=0,
                                    pattern=[[1, P]], channel_multiplier=-1).then_inc(s_const, 1)

            def rstds(S, w, m, p):
                g = 2 * m + p
                moments, steps, used = (("stats", "rstd", "xn"), ("st2", "rs2", "xn2"))[w]
                pool.wait_ge(S[moments], 2 * g + 2)
                nc.gpsimd.tensor_scalar(nmean[:, w, p], mv[:, w, p, :, 0], -1.0, None, ALU.mult)
                nc.gpsimd.tensor_scalar(veps[:, w, p], mv[:, w, p, :, 1], EPS, None, ALU.add).then_inc(S[steps], 1)
                pool.wait_ge(S[steps], 3 * g + 1)
                after(pool, S[used], g - 1)
                nc.gpsimd.tensor_tensor(rstd[:, w, p], veps[:, w, p], neg_half[:], ALU.pow).then_inc(S[steps], 1)
                pool.wait_ge(S[steps], 3 * g + 2)
                nc.gpsimd.tensor_tensor(nmr[:, w, p], nmean[:, w, p], rstd[:, w, p], ALU.mult).then_inc(S[steps], 1)
                pool.wait_ge(S[steps], 3 * g + 3)

            def normalize(w, g, tiles_of_group):
                p = g % 2
                for j in tiles_of_group:
                    last = nc.gpsimd.tensor_scalar(xn[w][p][:, j], xres[:, g * GT + j], rstd[:, w, p, j:j + 1],
                                                   nmr[:, w, p, j:j + 1], ALU.mult, ALU.add)
                return last

            def norm1(l, S, m, p):
                g = 2 * m + p
                rstds(S, 0, m, p)
                after(pool, S["xT"], g - 1)
                normalize(0, g, range(NA[l], GT)).then_inc(S["xnp"], 1)

            def norm2(l, S, m, p):
                g = 2 * m + p
                rstds(S, 1, m, p)
                after(pool, S["x2T"], g - 1)
                after(pool, s_rows[l][p], 16 * m)
                normalize(1, g, range(NA[l], GT)).then_inc(S["xn2p"], 1)

            def z_dot_q(k, p):
                pool.wait_ge(AS["z"], k + 1)
                pool.wait_ge(AS["phi"], k + 1)
                after(pool, AS["y"], k - 1)
                nc.gpsimd.tensor_tensor(op[p][0:H, :], zT[p][:], qT[p][:], ALU.mult).then_inc(AS["zq"], 1)

            for l in range(2):
                S = (AS, BS)[l]
                norm1(l, S, 0, 0)
                for k in range(NG + 2):
                    nxt, old = live(k // 2, k % 2, -1), live(k // 2, k % 2, 2)
                    if old:
                        norm2(l, S, *old)
                    if nxt:
                        norm1(l, S, *nxt)
                    if l == 0 and k < NG:
                        z_dot_q(k, k % 2)
                if l == 0:
                    nc.gpsimd.iota(rev8[:], pattern=[[-1, E]], base=E, channel_multiplier=0,
                                   allow_small_or_imprecise_dtypes=True)
                    nc.gpsimd.iota(iota_p[:], pattern=[[1, P]], base=0, channel_multiplier=0,
                                   allow_small_or_imprecise_dtypes=True)
                    nc.gpsimd.iota(part1[:], pattern=[[0, 1]], base=1, channel_multiplier=1,
                                   allow_small_or_imprecise_dtypes=True)
                    nc.gpsimd.iota(tile_base[:], pattern=[[P, NT], [0, ST]], base=0, channel_multiplier=0,
                                   allow_small_or_imprecise_dtypes=True)
                    nc.gpsimd.iota(spare[:], pattern=[[P, ST]], base=TOK + 1, channel_multiplier=1,
                                   allow_small_or_imprecise_dtypes=True)
                    nc.gpsimd.memset(restart[:], 1.0).then_inc(s_memset, 1)
                    pool.wait_ge(s_memset, 2)
                    nc.gpsimd.memset(restart[:, :, 0:1], 0.0).then_inc(s_const, 1)

                for p in range(2):
                    pool.wait_ge(s_rows[l][p], 16 * (NG // 2))
                pool.wait_ge(s_xrows[l], 16 * NG)
                pool.wait_ge(s_idx[l], 1)

                def gather(i):
                    after(pool, s_ys[l], i - ND + 1)
                    pool.indirect_dma_start(xs[i % ND][:], None, rows_dram[l],
                                            bass.IndirectOffsetOnAxis(ap=gidx[:, i:i + 1], axis=0)
                                            ).then_inc(s_gat[l][i % ND], 16)

                def scatter(i):
                    pool.wait_ge(s_ys[l], i + 1)
                    pool.indirect_dma_start(x_new[l], bass.IndirectOffsetOnAxis(ap=sidx[:, i:i + 1], axis=0),
                                            ys[i % ND][:], None, bounds_check=TOK - 1, oob_is_err=False
                                            ).then_inc(s_sct[l][i % ND], 16)

                for i in range(ND):
                    gather(i)
                for i in range(ST):
                    scatter(i)
                    if i + ND < ST:
                        gather(i + ND)

        @block.scalar
        def _(act):
            act.dma_start(wvk[:, 0:H], w_v).then_inc(s_wattn, 16)
            act.dma_start(wvk[:, H:2 * H], w_k).then_inc(s_wattn, 16)
            act.dma_start(wq[:], w_q).then_inc(s_wattn, 16)
            act.wait_ge(s_zeroed, 1)
            act.dma_start(wox[H:P, 0:D], w_o).then_inc(s_wattn, 16)

            def evac_xT(S, m, p, dst, read):
                act.wait_ge(S["xT"], 2 * m + p + 1)
                after(act, *read)
                nc.scalar.copy(dst[:], bank[0][:]).then_inc(S["xTe"], 1)

            def evac_x2T(S, m, p):
                g = 2 * m + p
                act.wait_ge(S["x2T"], g + 1)
                after(act, S["logits"], g)
                nc.scalar.copy(xn2T[:], bank[X2_BANK[S is BS]][:]).then_inc(S["x2Te"], 1)

            def norm(l, w, m, p):
                S = (AS, BS)[l]
                g = 2 * m + p
                done, steps, read = (("xn", "rstd", "xT"), ("xn2", "rs2", "x2T"))[w]
                act.wait_ge(S[steps], 3 * g + 3)
                after(act, S[read], g - 1)
                if w == 1:
                    after(act, s_rows[l][p], 16 * m)
                settle(act, g)
                for j in range(NA[l]):
                    src = xres[:, bass.ds(g * GT + j, 1), :].rearrange("p o d -> p (o d)")
                    last = nc.scalar.activation(xn[w][p][:, j], src, ACT.Identity, bias=nmr[:, w, p, j:j + 1],
                                                scale=rstd[:, w, p, j:j + 1])
                last.then_inc(S[done], 1)

            def attn_slot(m, p):
                k = 2 * m + p
                if live(m, p, 0):
                    evac_xT(AS, m, p, xnT[0], (AS["qp"], k))
                    act.wait_ge(AS["vkp"], k + 1)
                    after(act, AS["phik"], k)
                    nc.scalar.activation(ex[H:P, :], bank[1][H:P, :], ACT.Exp)
                    nc.scalar.activation(rl[H:P, :], bank[1][H:P, :], ACT.Relu).then_inc(AS["relk"], 1)
                    after(act, AS["o"], k - 1)
                    nc.scalar.copy(vk[p][0:H, :], bank[1][0:H, :]).then_inc(AS["v"], 1)
                    act.wait_ge(AS["qp"], k + 1)
                    after(act, AS["phi"], k)
                    nc.scalar.activation(ex[0:H, :], bank[2][0:H, :], ACT.Exp)
                    nc.scalar.activation(rl[0:H, :], bank[2][0:H, :], ACT.Relu).then_inc(AS["relq"], 1)
                if live(m, p, 1):
                    q = live(m, p, 1)[1]
                    act.wait_ge(AS["o"], k)
                    after(act, AS["y"], k - 2)
                    nc.scalar.copy(op[q][H:P, :], bank[5][H:P, :]).then_inc(AS["oe"], 1)
                if live(m, p, 2):
                    norm(0, 1, *live(m, p, 2))
                if live(m, p, 0):
                    act.wait_ge(AS["kvT"], k + 1)
                    nc.scalar.copy(kv[p][:], bank[3][:].rearrange("p (j c) -> p j c", j=GT)).then_inc(AS["kv"], 1)
                if live(m, p, 2):
                    evac_x2T(AS, *live(m, p, 2))
                if live(m, p, -1):
                    norm(0, 0, *live(m, p, -1))

            def mix_slot(m, p):
                k = 2 * m + p
                if live(m, p, 0):
                    evac_xT(BS, m, p, xnT[p], (BS["mix"], k - 1))
                if live(m, p, -1):
                    norm(1, 0, *live(m, p, -1))
                if live(m, p, 2):
                    norm(1, 1, *live(m, p, 2))
                if live(m, p, 0):
                    act.wait_ge(BS["mix"], k + 1)
                    after(act, BS["vm"], k)
                    for i in range(2):
                        src = bank[(1, 4)[p] + i][:].rearrange("t (j w d) -> t j w d", j=2, w=2)[:, :, 1]
                        last = nc.scalar.activation(sg[:, 2 * i:2 * i + 2], src, ACT.Sigmoid)
                    last.then_inc(BS["sig"], 1)
                if live(m, p, 2):
                    evac_x2T(BS, *live(m, p, 2))

            for l in range(2):
                norm(l, 0, 0, 0)
                slots(act, (attn_slot, mix_slot)[l])
                act.wait_ge(s_route[l], 2)
                nc.scalar.activation(le[:], ld[:], ACT.Exp).then_inc(s_lexp[l], 1)

                act.wait_ge(s_etab[l], 1)
                if l == 0:
                    act.wait_ge(s_wmix, 16 * 6)
                    nc.scalar.activation(edec[:], vec[:, 0:1], ACT.Exp).then_inc(s_decay, 1)
                    act.wait_ge(s_decay, 1)
                    nc.scalar.activation(decay[:], edec[:], ACT.Exp, scale=-1.0).then_inc(s_decay, 1)
                    act.wait_ge(s_setup_dve, 2)

                def evac_xs(i, r, n):
                    act.wait_ge(s_xsT[l], i + 1)
                    after(act, s_hD[l], i - NB + 1)
                    nc.scalar.copy(xsT[r % NB][:], bank[r % 2][:, 0:P]).then_inc(s_xsTe[l], 1)

                def relu(i, r, n):
                    e = act.value_load(etab[0:1, bass.ds(i, 1)], min_val=0, max_val=E - 1)
                    act.wait_ge(s_hA[l], i + 1)
                    after(act, s_ye[l], i - NB + 1)
                    for c in range(C // 2):
                        last = nc.scalar.activation(hT[r % NB][:, c], bank[2 + r % 2][:, c * P:(c + 1) * P], ACT.Relu,
                                                    bias=b1T[:, bass.ds(e * C + c, 1)])
                    last.then_inc(s_rA[l], 1)

                def step(*at):
                    if ahead(*at, 2):
                        evac_xs(*ahead(*at, 2))
                    if ahead(*at, 1):
                        relu(*ahead(*at, 1))

                evac_xs(0, 0, 0)
                evac_xs(1, 1, 0)
                relu(0, 0, 0)
                slot_tiles(act, step)

        @block.vector
        def _(dve):
            def tile_of(g, j):
                return xres[:, bass.ds(g * GT + j, 1), :].rearrange("p o d -> p (o d)")

            def stats_of(S, w, m, p):
                g = 2 * m + p
                after(dve, S[("stats", "st2")[w]], 2 * g)
                settle(dve, g)
                for j in range(GT):
                    last = nc.vector.bn_stats(stats[:, w, j], tile_of(g, j))
                last.then_inc(S[("stats", "st2")[w]], 1)

            def moments(S, w, m, p):
                g = 2 * m + p
                dve.wait_ge(S[("stats", "st2")[w]], 2 * g + 1)
                for n in (("xn", "xnp"), ("xn2", "xn2p"))[w]:
                    after(dve, S[n], g - 1)
                settle(dve, g)
                for j in range(GT):
                    last = nc.vector.bn_aggr(mv[:, w, p, j], stats[:, w, j])
                last.then_inc(S[("stats", "st2")[w]], 1)

            def first_stats(l, m, p):
                dve.wait_ge(s_x_in[l][p], 16 * (m + 1))
                stats_of((AS, BS)[l], 0, m, p)

            def logits_out(S, m, p):
                g = 2 * m + p
                dve.wait_ge(S["logits"], g + 1)
                nc.vector.tensor_tensor(lg[:, tiles(g), :],
                                        bank[LG_BANK[S is BS]][:, 0:GT * E].rearrange("p (j e) -> p j e", j=GT),
                                        rtb[:].unsqueeze(1).to_broadcast([P, GT, E]), ALU.add).then_inc(S["lgs"], 1)

            def attn_slot(m, p):
                k = 2 * m + p
                back = live(m, p, 1)
                if back:
                    mm, q = back
                    dve.wait_ge(AS["scores"], k)
                    after(dve, AS["o"], k - 1)
                    nc.vector.tensor_tensor(am[:], bank[4][:].rearrange("p (j t) -> p j t", j=GT),
                                            causal[:].unsqueeze(1).to_broadcast([P, GT, P]), ALU.mult
                                            ).then_inc(AS["am"], 1)
                    dve.wait_ge(AS["upd"], k)
                    n = GT if q == 0 else GT - 1
                    upd = bank[5][0:H, 0:H * n].rearrange("v (j k) -> v j k", j=n)
                    if q == 0:
                        nc.vector.tensor_copy(state[0][:], upd).then_inc(AS["state"], 1)
                    else:
                        dve.wait_ge(AS["state"], k - 1)
                        nc.vector.tensor_tensor(state[1][:, 0:n], upd,
                                                state[0][:, GT - 1:GT].to_broadcast([H, n, H]), ALU.add
                                                ).then_inc(AS["state"], 1)
                nxt = live(m, p, -1)
                if nxt:
                    first_stats(0, *nxt)
                if live(m, p, 0):
                    dve.wait_ge(AS["relk"], k + 1)
                    nc.vector.scalar_tensor_tensor(out=vk[p][H:P, :], in0=ex[H:P, :], scalar=1.0, in1=rl[H:P, :],
                                                   op0=ALU.min, op1=ALU.add).then_inc(AS["phik"], 1)
                if nxt:
                    moments(AS, 0, *nxt)
                if live(m, p, 0):
                    dve.wait_ge(AS["relq"], k + 1)
                    after(dve, AS["zq"], k - 1)
                    nc.vector.scalar_tensor_tensor(out=qT[p][:], in0=ex[0:H, :], scalar=1.0, in1=rl[0:H, :],
                                                   op0=ALU.min, op1=ALU.add).then_inc(AS["phi"], 1)
                    dve.wait_ge(AS["phik"], k + 1)
                    after(dve, AS["z"], k)
                    nc.vector.tensor_tensor_scan(zT[p][:], ones_col[H:P, 0:1].to_broadcast([H, GW]), vk[p][H:P, :],
                                                 0.0 if p == 0 else zT[0][:, GW - 1:GW], ALU.mult, ALU.add
                                                 ).then_inc(AS["z"], 1)
                if back:
                    dve.wait_ge(AS["y"], k)
                    outs = [bank[6 + i][:, 0:2 * YC].rearrange("p (j c) -> p j c", j=2) for i in range(2)]
                    for i in range(2):
                        last = nc.vector.tensor_scalar(rden[:, 0, 2 * i:2 * i + 2], outs[i][:, :, D], 1e-6, None,
                                                       ALU.max)
                    last.then_inc(AS["dmax"], 1)
                    dve.wait_ge(AS["dmax"], k)
                    nc.vector.reciprocal(rden[:, 1], rden[:, 0]).then_inc(AS["rden"], 1)
                    dve.wait_ge(AS["rden"], k)
                    for j in range(GT):
                        t = tile_of(k - 1, j)
                        last = nc.vector.scalar_tensor_tensor(out=t, in0=outs[j // 2][:, j % 2, 0:D],
                                                              scalar=rden[:, 1, j:j + 1], in1=t,
                                                              op0=ALU.mult, op1=ALU.add)
                    last.then_inc(AS["xnew"], 1)
                    dve.wait_ge(AS["xnew"], k)
                    stats_of(AS, 1, mm, q)
                if live(m, p, 2):
                    logits_out(AS, *live(m, p, 2))
                if back:
                    moments(AS, 1, mm, q)

            def mix_slot(m, p):
                k = 2 * m + p
                back = live(m, p, 1)
                if live(m, p, -1):
                    first_stats(1, *live(m, p, -1))
                if back:
                    mm, q = back
                    dve.wait_ge(BS["sig"], k)
                    after(dve, BS["xnew"], k - 1)
                    for i in range(2):
                        val = bank[(1, 4)[q] + i][:].rearrange("t (j w d) -> t j w d", j=2, w=2)[:, :, 0]
                        last = nc.vector.tensor_tensor(tm[:, 2 * i:2 * i + 2], sg[:, 2 * i:2 * i + 2], val, ALU.mult)
                    last.then_inc(BS["vm"], 1)
                if live(m, p, -1):
                    moments(BS, 0, *live(m, p, -1))
                if live(m, p, 0):
                    dve.wait_ge(BS["xTe"], k + 1)
                    after(dve, BS["mix"], k - 1)
                    after(dve, BS["scan"], k)
                    if p == 1:
                        nc.vector.tensor_copy(sc[1][:, 0:1], sc[0][:, GW:GW + 1])
                    nc.vector.tensor_tensor_scan(sc[p][:, 1:1 + GW], decay[:, 0:1].to_broadcast([P, GW]), xnT[p][:],
                                                 0.0 if p == 0 else sc[0][:, GW:GW + 1], ALU.mult, ALU.add
                                                 ).then_inc(BS["scan"], 1)
                if back:
                    dve.wait_ge(BS["vm"], k)
                    nc.vector.tensor_tensor(xres[:, tiles(k - 1), :], xres[:, tiles(k - 1), :], tm[:], ALU.add
                                            ).then_inc(BS["xnew"], 1)
                if back:
                    dve.wait_ge(BS["xnew"], k)
                    stats_of(BS, 1, mm, q)
                if live(m, p, 3):
                    logits_out(BS, *live(m, p, 3))
                if back:
                    moments(BS, 1, mm, q)

            def route(l):
                n = [0]

                def step(ins):
                    n[0] += 1
                    ins.then_inc(s_route[l], 1)
                    dve.wait_ge(s_route[l], n[0])

                def per_tile(a, k=E):
                    return a.unsqueeze(2).to_broadcast([P, NT, k])

                dve.wait_ge((AS, BS)[l]["lgs"], NG)
                dve.wait_ge(s_const, 2)
                step(nc.vector.tensor_reduce(mx[:], lg[:], AX_X, ALU.max))
                step(nc.vector.tensor_tensor(ld[:], lg[:], per_tile(mx[:]), ALU.subtract))
                step(nc.vector.scalar_tensor_tensor(out=rv[:], in0=ld[:], scalar=0.0,
                                                    in1=rev8[:].unsqueeze(1).to_broadcast([P, NT, E]),
                                                    op0=ALU.is_equal, op1=ALU.mult))
                step(nc.vector.tensor_reduce(top[:], rv[:], AX_X, ALU.max))
                nc.vector.tensor_tensor(oh[:], rev8[:].unsqueeze(1).to_broadcast([P, NT, E]), per_tile(top[:]),
                                        ALU.is_equal).then_inc(s_oh[l], 1)
                dve.wait_ge(s_lexp[l], 1)
                step(nc.vector.tensor_reduce(sm[:], le[:], AX_X, ALU.add))
                nc.vector.reciprocal(gate[:], sm[:])
                dve.wait_ge(s_count[l], 1)
                step(nc.vector.tensor_copy(tot[:], bank[2][:, 0:NT * E].rearrange("p (t e) -> p e t", e=E)))
                step(nc.vector.tensor_tensor_scan(cum[:].rearrange("p e t -> p (e t)"),
                                                  restart[:].rearrange("p e t -> p (e t)"),
                                                  tot[:].rearrange("p e t -> p (e t)"), 0.0, ALU.mult, ALU.add))
                nc.vector.tensor_tensor(exc[:], cum[:], tot[:], ALU.subtract)
                step(nc.vector.tensor_scalar(etiles[:, 0], cum[:, :, NT - 1], 1.0 / P, (P - 1) / 2 / P, ALU.mult, ALU.add))
                step(nc.vector.tensor_scalar(etiles[:, 1], etiles[:, 0], ROUND, -ROUND, ALU.add, ALU.add))
                step(nc.vector.tensor_tensor_scan(etiles[:, 2], ones_col[:, 0:1].to_broadcast([P, E]), etiles[:, 1],
                                                  0.0, ALU.mult, ALU.add))
                step(nc.vector.tensor_tensor(ebase[:], etiles[:, 2], etiles[:, 1], ALU.subtract))
                step(nc.vector.tensor_tensor(ecmp[:], iota_p[0:1, 0:ST].unsqueeze(2).to_broadcast([1, ST, E]),
                                             etiles[0:1, 2].unsqueeze(1).to_broadcast([1, ST, E]), ALU.is_ge))
                step(nc.vector.tensor_reduce(ecnt[:], ecmp[:], AX_X, ALU.add))
                nc.vector.tensor_scalar(etab[0:1, 0:ST], ecnt[:], float(E - 1), None, ALU.min).then_inc(s_etab[l], 1)
                step(nc.vector.scalar_tensor_tensor(out=slot_e[:], in0=ebase[:].unsqueeze(2).to_broadcast([P, E, NT]),
                                                    scalar=float(P), in1=exc[:], op0=ALU.mult, op1=ALU.add))
                step(nc.vector.tensor_tensor(tot[:], bank[1][:, 0:NT * E].rearrange("p (t e) -> p e t", e=E), slot_e[:],
                                             ALU.add))
                step(nc.vector.tensor_tensor(cum[:], tot[:], oh[:].rearrange("p t e -> p e t"), ALU.mult))
                step(nc.vector.tensor_reduce(pos[:], cum[:].rearrange("p e t -> p t e"), AX_X, ALU.add))
                step(nc.vector.tensor_scalar(hi[:, 0], pos[:], 1.0 / P, -(P - 1) / 2 / P, ALU.mult, ALU.add))
                step(nc.vector.tensor_scalar(hi[:, 1], hi[:, 0], ROUND, -ROUND, ALU.add, ALU.add))
                step(nc.vector.scalar_tensor_tensor(out=lo[:], in0=hi[:, 1], scalar=-float(P), in1=pos[:],
                                                    op0=ALU.mult, op1=ALU.add))
                step(nc.vector.tensor_tensor(hi1h[:], iota_p[:, 0:ST].unsqueeze(1).to_broadcast([P, NT, ST]),
                                             per_tile(hi[:, 1], ST), ALU.is_equal))
                nc.vector.tensor_scalar(hid[:, :, 0], hi1h[:], part1[:, 0:1], None, ALU.mult)
                nc.vector.tensor_tensor(hid[:, :, 1], hi1h[:], tile_base[:], ALU.mult).then_inc(s_onehots[l], 1)
                for q in range(4):
                    t = slice(NT // 4 * q, NT // 4 * (q + 1))
                    nc.vector.tensor_tensor(lo1h[:, t], iota_p[:].unsqueeze(1).to_broadcast([P, NT // 4, P]),
                                            lo[:, t].unsqueeze(2).to_broadcast([P, NT // 4, P]), ALU.is_equal
                                            ).then_inc(s_onehots[l], 1)
                dve.wait_ge(s_inv[l], 1)
                step(nc.vector.tensor_copy(ivh[:], bank[4][:, 0:ST]))
                step(nc.vector.tensor_tensor(iv[:], bank[4][:, ST:2 * ST], ivh[:], ALU.add))
                nc.vector.tensor_scalar(gidx[:], iv[:], -1.0, 0.0, ALU.add, ALU.max)
                step(nc.vector.scalar_tensor_tensor(out=ivz[:], in0=iv[:], scalar=0.0, in1=spare[:],
                                                    op0=ALU.is_equal, op1=ALU.mult))
                nc.vector.scalar_tensor_tensor(out=sidx[:], in0=iv[:], scalar=-1.0, in1=ivz[:],
                                               op0=ALU.add, op1=ALU.add).then_inc(s_idx[l], 1)

            def gates(l):
                for w in range(3):
                    whole = gate if w == 0 else grest[:, w - 1]
                    nc.vector.tensor_copy(gpart[:, w], whole[:]).then_inc(s_gates[l], 1)
                    dve.wait_ge(s_gates[l], 2 * w + 1)
                    if w < 2:
                        nc.vector.tensor_tensor(grest[:, w], whole[:], gpart[:, w], ALU.subtract
                                                ).then_inc(s_gates[l], 1)
                        dve.wait_ge(s_gates[l], 2 * w + 2)
                for w in range(3):
                    last = nc.vector.tensor_tensor(hig[:, :, w], hi1h[:],
                                                   gpart[:, w].unsqueeze(2).to_broadcast([P, NT, ST]), ALU.mult)
                last.then_inc(s_gates[l], 1)

            def gates_out(l):
                dve.wait_ge(s_inv[l], 2)
                nc.vector.tensor_copy(gsum[:, 0], bank[3][:, 0:ST]).then_inc(s_gates[l], 1)
                dve.wait_ge(s_gates[l], 7)
                nc.vector.tensor_tensor(gsum[:, 1], bank[3][:, ST:2 * ST], gsum[:, 0], ALU.add).then_inc(s_gates[l], 1)
                dve.wait_ge(s_gates[l], 8)
                nc.vector.tensor_tensor(gslot[:], bank[3][:, 2 * ST:3 * ST], gsum[:, 1], ALU.add
                                        ).then_inc(s_gates[l], 1)

            def mix_weights():
                nc.vector.tensor_copy(b1T[:], bank[7][:, 2 * P:2 * P + E * C])
                nc.vector.tensor_scalar(mix_c[:], vec[:, 1:3], -1.0, 1.0, ALU.mult, ALU.add).then_inc(s_setup_dve, 1)
                dve.wait_ge(s_setup_pe, 2)
                dve.wait_ge(s_setup_dve, 2)
                for w in range(2):
                    src = (bank[6][:, 0:P], bank[7][:, P:2 * P])[w]
                    nc.vector.tensor_scalar(wx[:, w], src, vec[:, 1 + w:2 + w], None, ALU.mult)
                    last = nc.vector.tensor_scalar(wp[:, w], src, mix_c[:, w:w + 1], None, ALU.mult)
                last.then_inc(s_setup_dve, 1)

            def experts(l):
                def expert(i):
                    return dve.value_load(etab[0:1, bass.ds(i, 1)], min_val=0, max_val=E - 1)

                def relu(i, r, n):
                    e = expert(i)
                    dve.wait_ge(s_hD[l], i + 1)
                    after(dve, s_ye[l], i - NB + 1)
                    for c in range(C // 2, C):
                        last = nc.vector.tensor_scalar(hT[r % NB][:, c], bank[4 + r % 2][:, (c - C // 2) * P:(c - C // 2 + 1) * P],
                                                       b1T[:, bass.ds(e * C + c, 1)], 0.0, ALU.add, ALU.max)
                    last.then_inc(s_rD[l], 1)

                def before_y(i, r, n):
                    e = expert(i)
                    dve.wait_ge(s_gat[l][r % ND], 16 * (n + 1))
                    nc.vector.scalar_tensor_tensor(out=xs[r % ND][:, D:], in0=b2b[:, bass.ds(e, 1), :].rearrange("p o d -> p (o d)"),
                                                   scalar=gslot[:, bass.ds(i, 1)], in1=xs[r % ND][:, D:],
                                                   op0=ALU.mult, op1=ALU.add).then_inc(s_pre[l], 1)

                def add_y(i, r, n):
                    b = r % ND
                    dve.wait_ge(s_ye[l], i + 1)
                    dve.wait_ge(s_pre[l], i + 1)
                    after(dve, s_sct[l][b], 16 * n)
                    nc.vector.scalar_tensor_tensor(out=ys[b][:], in0=bank[6 + r % 2][:, 0:P],
                                                   scalar=gslot[:, bass.ds(i, 1)], in1=xs[b][:, D:],
                                                   op0=ALU.mult, op1=ALU.add).then_inc(s_ys[l], 1)

                def step(*at):
                    if ahead(*at, 1):
                        relu(*ahead(*at, 1))
                        before_y(*ahead(*at, 1))
                    add_y(*at)

                dve.wait_ge(s_etab[l], 1)
                if l == 0:
                    dve.wait_ge(s_setup_pe, 1)
                    nc.vector.tensor_copy(rwoT[:], bank[7][:, 0:P]).then_inc(s_setup_dve, 1)
                gates(l)
                if l == 0:
                    mix_weights()
                gates_out(l)
                dve.wait_ge(s_gates[l], 9)
                dve.wait_ge(s_w2, 16 * (1 + E))
                relu(0, 0, 0)
                before_y(0, 0, 0)
                slot_tiles(dve, step)

            nc.vector.memset(wox[:], 0.0).then_inc(s_zeroed, 1)
            dve.wait_ge(s_zeroed, 1)
            nc.vector.memset(wox[0:H, D:YC], 1.0).then_inc(s_zeroed, 1)
            nc.vector.memset(sc[0][:, 0:1], 0.0)
            first_stats(0, 0, 0)
            moments(AS, 0, 0, 0)

            slots(dve, attn_slot)
            route(0)
            experts(0)
            first_stats(1, 0, 0)
            moments(BS, 0, 0, 0)
            slots(dve, mix_slot)
            logits_out(BS, NG // 2 - 1, 1)
            route(1)
            experts(1)

        @block.tensor
        def _(pe):
            def transpose_x(S, m, p):
                g = 2 * m + p
                pe.wait_ge(S["xn"], g + 1)
                pe.wait_ge(S["xnp"], g + 1)
                if S is AS:
                    after(pe, S["x2Te"], g - 2)
                else:
                    after(pe, S["xTe"], g)
                for j in range(GT):
                    last = nc.tensor.transpose(bank[0][:, j * P:(j + 1) * P], xn[0][p][:, j], ident[:])
                last.then_inc(S["xT"], 1)

            def transpose_x2(S, m, p):
                g = 2 * m + p
                pe.wait_ge(S["xn2"], g + 1)
                pe.wait_ge(S["xn2p"], g + 1)
                if S is AS:
                    pe.wait_ge(S["xTe"], min(g + 3, NG) if isinstance(g, int) else g + 3)
                else:
                    after(pe, S["x2Te"], g)
                for j in range(GT):
                    last = nc.tensor.transpose(bank[X2_BANK[S is BS]][:, j * P:(j + 1) * P], xn[1][p][:, j], ident[:])
                last.then_inc(S["x2T"], 1)

            def logits(S, m, p):
                g = 2 * m + p
                pe.wait_ge(S["x2Te"], g + 1)
                after(pe, S["lgs"], g)
                if S is AS:
                    pe.wait_ge(S["kv"], min(g + 3, NG) if isinstance(g, int) else g + 3)
                for j in range(GT):
                    last = nc.tensor.matmul(bank[LG_BANK[S is BS]][:, E * j:E * (j + 1)], xn2T[:, j * P:(j + 1) * P],
                                            rtw[:], start=True, stop=True)
                last.then_inc(S["logits"], 1)

            def attn_slot(m, p):
                k = 2 * m + p
                cur, back, old = live(m, p, 0), live(m, p, 1), live(m, p, 2)
                if cur:
                    transpose_x(AS, m, p)
                if back:
                    mm, q = back
                    pe.wait_ge(AS["phi"], k)
                    after(pe, AS["am"], k - 1)
                    for j in range(GT):
                        t = slice(j * P, (j + 1) * P)
                        last = nc.tensor.matmul(bank[4][:, t], vk[q][0:H, t], qT[q][:, t], start=True, stop=True)
                    last.then_inc(AS["scores"], 1)
                if cur:
                    pe.wait_ge(AS["xTe"], k + 1)
                    after(pe, AS["relq"], k)
                    after(pe, AS["v"], k)
                    nc.tensor.matmul(bank[1][:], wvk[:], xnT[0][:], start=True, stop=True).then_inc(AS["vkp"], 1)
                if back:
                    pe.wait_ge(AS["kv"], k)
                    after(pe, AS["state"], k - 1)
                    settle(pe, k)
                    n = GT if q == 0 else GT - 1
                    for j in range(n):
                        last = nc.tensor.matmul(bank[5][0:H, H * j:H * n].rearrange("v (i k) -> v i k", k=H),
                                                kv[q][:, j, 0:H],
                                                kv[q][:, j:j + 1, H:2 * H].to_broadcast([P, n - j, H]),
                                                start=(j == 0), stop=(j == n - 1))
                    last.then_inc(AS["upd"], 1)
                if cur:
                    nc.tensor.matmul(bank[2][0:H, :], wq[:], xnT[0][:], start=True, stop=True).then_inc(AS["qp"], 1)
                if back:
                    pe.wait_ge(AS["am"], k)
                    pe.wait_ge(AS["state"], k)
                    after(pe, AS["oe"], k - 1)
                    settle(pe, k)
                    for j in range(GT):
                        t = slice(j * P, (j + 1) * P)
                        first = q == 0 and j == 0
                        last = nc.tensor.matmul(bank[5][H:P, t], kv[q][:, j, H:2 * H], am[:, j], start=True, stop=first)
                        if not first:
                            before_t = state[q][:, j - 1] if j > 0 else state[0][:, GT - 1]
                            last = nc.tensor.matmul(bank[5][H:P, t], before_t, qT[q][:, t], start=False, stop=True)
                    last.then_inc(AS["o"], 1)
                if cur:
                    pe.wait_ge(AS["phik"], k + 1)
                    pe.wait_ge(AS["v"], k + 1)
                    after(pe, AS["kv"], k)
                    after(pe, AS["lgs"], k - 2)
                    for j in range(GT):
                        last = nc.tensor.transpose(bank[3][:, j * P:(j + 1) * P], vk[p][:, j * P:(j + 1) * P],
                                                   ident[:])
                    last.then_inc(AS["kvT"], 1)
                if back:
                    pe.wait_ge(AS["oe"], k)
                    pe.wait_ge(AS["zq"], k)
                    for j in range(GT):
                        last = nc.tensor.matmul(bank[6 + j // 2][:, YC * (j % 2):YC * (j % 2 + 1)],
                                                op[q][:, j * P:(j + 1) * P], wox[:], start=True, stop=True)
                    last.then_inc(AS["y"], 1)
                if old:
                    transpose_x2(AS, *old)
                    logits(AS, *old)

            def mix_slot(m, p):
                k = 2 * m + p
                cur, old = live(m, p, 0), live(m, p, 2)
                if cur:
                    transpose_x(BS, m, p)
                if live(m, p, 3):
                    logits(BS, *live(m, p, 3))
                if cur:
                    pe.wait_ge(BS["scan"], k + 1)
                    pe.wait_ge(BS["xTe"], k + 1)
                    after(pe, BS["vm"], k - 1)
                    for j in range(GT):
                        t = slice(j * P, (j + 1) * P)
                        o = bank[(1, 4)[p] + j // 2][:, 2 * P * (j % 2):2 * P * (j % 2 + 1)]
                        nc.tensor.matmul(o, xnT[p][:, t], wx[:].rearrange("p w d -> p (w d)"), start=True, stop=False)
                        last = nc.tensor.matmul(o, sc[p][:, t], wp[:].rearrange("p w d -> p (w d)"),
                                                start=False, stop=True)
                    last.then_inc(BS["mix"], 1)
                if old:
                    transpose_x2(BS, *old)

            def setup_transposes():
                pe.wait_ge(s_wmix, 16 * 6)
                pe.wait_ge(s_b1, 16)
                pe.wait_ge(AS["xnew"], NG)
                nc.tensor.transpose(bank[7][:, 0:P], rwo[:], ident[:])
                nc.tensor.transpose(bank[7][:, P:2 * P], rwr[:], ident[:])
                nc.tensor.transpose(bank[7][:, 2 * P:2 * P + E * C], b1n[:], ident[0:E * C, 0:E * C]
                                    ).then_inc(s_setup_pe, 1)

            def setup_product():
                pe.wait_ge(s_setup_dve, 1)
                nc.tensor.matmul(bank[6][:, 0:P], rwv[:], rwoT[:], start=True, stop=True).then_inc(s_setup_pe, 1)

            def gates(l):
                pe.wait_ge(s_gates[l], 6)
                for t in range(NT):
                    last = nc.tensor.matmul(bank[3][:, 0:3 * ST], lo1h[:, t], hig[:, t].rearrange("p w s -> p (w s)"),
                                            start=(t == 0), stop=(t == NT - 1))
                last.then_inc(s_inv[l], 1)

            def route(l):
                pe.wait_ge(s_oh[l], 1)
                ohf = oh[:].rearrange("p t e -> p (t e)")
                nc.tensor.matmul(bank[1][:, 0:NT * E], before[:], ohf, start=True, stop=True)
                nc.tensor.matmul(bank[2][:, 0:NT * E], ones_bf[:], ohf, start=True, stop=True).then_inc(s_count[l], 1)
                for t in range(NT):
                    if t % (NT // 4) == 0:
                        pe.wait_ge(s_onehots[l], 2 + t // (NT // 4))
                    last = nc.tensor.matmul(bank[4][:, 0:2 * ST], lo1h[:, t], hid[:, t].rearrange("p w s -> p (w s)"),
                                            start=(t == 0), stop=(t == NT - 1))
                last.then_inc(s_inv[l], 1)

            def experts(l):
                def turn(i, r, n):
                    pe.wait_ge(s_gat[l][r % ND], 16 * (n + 1))
                    after(pe, s_xsTe[l], i - 1)
                    nc.tensor.transpose(bank[r % 2][:, 0:P], xs[r % ND][:, 0:D], ident[:]).then_inc(s_xsT[l], 1)

                def first(i, r, n):
                    pe.wait_ge(s_xsTe[l], i + 1)
                    pe.wait_ge(s_w1[l][r % ND], 16 * (n + 1))
                    for half, ready, used in ((0, s_hA[l], s_rA[l]), (1, s_hD[l], s_rD[l])):
                        after(pe, used, i - 1)
                        for c in range(C // 2):
                            f = (half * (C // 2) + c) * P
                            mm = nc.tensor.matmul(bank[2 + 2 * half + r % 2][:, c * P:(c + 1) * P],
                                                  w1s[r % ND][:, f:f + P], xsT[r % NB][:], start=True, stop=True)
                        mm.then_inc(ready, 1)

                def second(i, r, n):
                    e = pe.value_load(etab[0:1, bass.ds(i, 1)], min_val=0, max_val=E - 1)
                    pe.wait_ge(s_rA[l], i + 1)
                    pe.wait_ge(s_rD[l], i + 1)
                    after(pe, s_ys[l], i - 1)
                    for c in range(C):
                        mm = nc.tensor.matmul(bank[6 + r % 2][:, 0:P], hT[r % NB][:, c],
                                              w2s[:, bass.ds(e, 1), c, :].rearrange("p o d -> p (o d)"),
                                              start=(c == 0), stop=(c == C - 1))
                    mm.then_inc(s_ye[l], 1)

                def step(*at):
                    if ahead(*at, 2):
                        turn(*ahead(*at, 2))
                    if ahead(*at, 1):
                        first(*ahead(*at, 1))
                    second(*at)

                pe.wait_ge(s_etab[l], 1)
                if l == 0:
                    setup_product()
                gates(l)
                if l == 0:
                    pe.wait_ge(s_setup_dve, 3)
                    pe.wait_ge(s_w2, 16 * (1 + E))
                turn(0, 0, 0)
                turn(1, 1, 0)
                pe.wait_ge(s_gates[l], 9)
                first(0, 0, 0)
                slot_tiles(pe, step)

            pe.wait_ge(s_const, 1)
            pe.wait_ge(s_wattn, 64)
            pe.wait_ge(s_zeroed, 2)
            pe.wait_ge(s_router, 32)

            slots(pe, attn_slot)
            setup_transposes()
            route(0)
            experts(0)
            slots(pe, mix_slot)
            logits(BS, NG // 2 - 1, 1)
            route(1)
            experts(1)


_INS = ['L0_attn_a_x', 'L0_attn_a_W_q', 'L0_attn_a_W_k', 'L0_attn_a_W_v', 'L0_attn_a_W_o',
        'L0_attn_b_time_decay', 'L0_attn_b_time_mix_v', 'L0_attn_b_time_mix_r',
        'L0_attn_b_Wv', 'L0_attn_b_Wr', 'L0_attn_b_Wo',
        'L0_ffn_router_W', 'L0_ffn_router_b', 'L0_ffn_W1', 'L0_ffn_b1', 'L0_ffn_W2', 'L0_ffn_b2']


def kernel(**inputs):
    import numpy as _np
    import concourse.bacc as _bacc
    from concourse import mybir as _mybir
    from concourse.bass_utils import run_bass_kernel_spmd as _run

    nc = _bacc.Bacc("TRN2", target_bir_lowering=False, num_devices=1)
    arrays, args = {}, []
    for name in _INS:
        a = _np.ascontiguousarray(inputs[name])
        arrays[f"in_{name}"] = a
        args.append(nc.dram_tensor(f"in_{name}", a.shape, _mybir.dt.from_np(a.dtype), kind="ExternalInput").ap())
    out = nc.dram_tensor("out", inputs['L0_attn_a_x'].shape, _mybir.dt.float32, kind="ExternalOutput").ap()
    hybrid_block(nc, *args, out)
    r = _run(nc, [arrays], core_ids=[0])
    return r.results[0]["out"]
```

```python
from contextlib import ExitStack

import concourse.bass as bass
from concourse import mybir

ALU = mybir.AluOpType
ACT = mybir.ActivationFunctionType
F32 = mybir.dt.float32
BF16 = mybir.dt.bfloat16
I32 = mybir.dt.int32
AX_X = mybir.AxisListType.X

P = 128
GT = 4
EPS = 1e-5
ROUND = 12582912.0
NB = 3
ND = 12
NW = 6


def after(eng, sem, n):
    if not isinstance(n, int) or n > 0:
        eng.wait_ge(sem, n)


def hybrid_block(nc, x, w_q, w_k, w_v, w_o, time_decay, mix_v, mix_r, rw_v, rw_r, rw_o,
                 router_w, router_b, w1, b1, w2, b2, out):
    B, T, D = x.shape
    H = w_q.shape[1]
    NA = (2, 3)
    E, _, DF = w1.shape
    assert D == P and 2 * H == P
    TOK = B * T
    NT = TOK // P
    NG = NT // GT
    GPB = T // P // GT
    assert GPB == 2 and NG == 2 * B
    C = DF // P
    ST = NT + E - 1
    UN = 12
    assert ST % UN >= 2 and UN % ND == 0 and UN % NW == 0 and UN % NB == 0
    GW = GT * P
    YC = P + 1

    xt = x.rearrange("b t d -> (b t) d").rearrange("(n p) d -> p n d", p=P)
    RW = 2 * D + 8
    rows_dram = [nc.dram_tensor(f"rows{l}", [TOK, RW], F32).ap() for l in range(2)]
    x_mid = nc.dram_tensor("x_mid", [TOK, D], F32).ap()
    x_new = [x_mid, out.rearrange("b t d -> (b t) d")]

    with ExitStack() as ctx:
        def sb(name, shape, dt=F32):
            return ctx.enter_context(nc.sbuf_tensor(name, shape, dt))

        def sem(name):
            return ctx.enter_context(nc.semaphore(name))

        bank = [ctx.enter_context(nc.psum_tensor(f"bank{i}", [P, 512], F32)) for i in range(8)]

        LG_BANK = (3, 6)
        X2_BANK = (0, 3)

        ident = sb("ident", [P, P])
        causal = sb("causal", [P, P])
        before = sb("before", [P, P], BF16)
        ones_bf = sb("ones_bf", [P, P], BF16)
        ones_col = sb("ones_col", [P, 1])
        neg_half = sb("neg_half", [P, GT])
        unread = sb("unread", [P, GT])
        rev8 = sb("rev8", [P, E])
        iota_p = sb("iota_p", [P, P])
        iota_bf = sb("iota_bf", [P, P], BF16)
        part1 = sb("part1", [P, 1])
        tile_base = sb("tile_base", [P, NT, ST], BF16)
        spare = sb("spare", [P, ST])
        restart = sb("restart", [P, E, NT])
        wvk = sb("wvk", [P, 2 * H])
        wq = sb("wq", [P, H])
        wox = sb("wox", [P, YC])
        vec = sb("vec", [P, 3])
        mix_c = sb("mix_c", [P, 2])
        edec = sb("edec", [P, 1])
        decay = sb("decay", [P, 1])
        rwv = sb("rwv", [P, P])
        rwr = sb("rwr", [P, P])
        rwo = sb("rwo", [P, P])
        rwoT = sb("rwoT", [P, P])
        wx = sb("wx", [P, 2, P])
        wp = sb("wp", [P, 2, P])
        rtw = sb("rtw", [P, E])
        rtb = sb("rtb", [P, E])
        b1n = sb("b1n", [E * C, P])
        b1T = sb("b1T", [P, E * C])
        b2b = sb("b2b", [P, E, D])
        w2s = sb("w2s", [P, E, C, D])
        xres = sb("xres", [P, NT, D])
        stats = sb("stats", [P, 2, GT, 6])
        mv = sb("mv", [P, 2, 2, GT, 2])
        nmean = sb("nmean", [P, 2, 2, GT])
        veps = sb("veps", [P, 2, 2, GT])
        rstd = sb("rstd", [P, 2, 2, GT])
        nmr = sb("nmr", [P, 2, 2, GT])
        xn = [[sb(f"xn{w}{p}", [P, GT, D]) for p in range(2)] for w in range(2)]
        xnT = [sb(f"xnT{p}", [P, GW]) for p in range(2)]
        xn2T = sb("xn2T", [P, GW])
        ex = sb("ex", [P, GW])
        rl = sb("rl", [P, GW])
        vk = [sb(f"vk{p}", [P, GW]) for p in range(2)]
        qT = [sb(f"qT{p}", [H, GW]) for p in range(2)]
        kv = [sb(f"kv{p}", [P, GT, 2 * H]) for p in range(2)]
        zT = [sb(f"zT{p}", [H, GW]) for p in range(2)]
        op = [sb(f"op{p}", [P, GW]) for p in range(2)]
        am = sb("am", [P, GT, P])
        state = [sb(f"state{p}", [H, GT, H]) for p in range(2)]
        rden = sb("rden", [P, 2, GT])
        sc = [sb(f"sc{p}", [P, 1 + GW]) for p in range(2)]
        sg = sb("sg", [P, GT, D])
        tm = sb("tm", [P, GT, D])
        lg = sb("lg", [P, NT, E])
        mx = sb("mx", [P, NT])
        ld = sb("ld", [P, NT, E])
        le = sb("le", [P, NT, E])
        sm = sb("sm", [P, NT])
        gate1 = sb("gate1", [P, NT])
        gate = sb("gate", [P, NT, RW - 2 * D])
        rv = sb("rv", [P, NT, E])
        top = sb("top", [P, NT])
        oh = sb("oh", [P, NT, E], BF16)
        tot = sb("tot", [P, E, NT])
        cum = sb("cum", [P, E, NT])
        exc = sb("exc", [P, E, NT])
        etiles = sb("etiles", [P, 3, E])
        ebase = sb("ebase", [P, E])
        slot_e = sb("slot_e", [P, E, NT])
        pos = sb("pos", [P, NT])
        hi = sb("hi", [P, NT])
        hi_bf = sb("hi_bf", [P, NT], BF16)
        lo = sb("lo", [P, NT])
        ecmp = sb("ecmp", [1, ST, E])
        ecnt = sb("ecnt", [1, ST])
        etab = sb("etab", [1, ST + 1], I32)
        lo1h = sb("lo1h", [P, NT, P], BF16)
        hi1h = sb("hi1h", [P, NT, ST], BF16)
        hid = sb("hid", [P, NT, 2, ST], BF16)
        ivh = sb("ivh", [P, ST])
        iv = sb("iv", [P, ST])
        ivz = sb("ivz", [P, ST])
        gidx = sb("gidx", [P, ST], I32)
        sidx = sb("sidx", [P, ST], I32)
        xs = [sb(f"xs{b}", [P, RW]) for b in range(ND)]
        xsT = [sb(f"xsT{b}", [P, P]) for b in range(NB)]
        w1s = [sb(f"w1s{b}", [P, DF]) for b in range(NW)]
        hT = [sb(f"hT{b}", [P, C, P]) for b in range(NB)]
        ys = [sb(f"ys{b}", [P, D]) for b in range(ND)]

        s_const = sem("s_const")
        s_memset = sem("s_memset")
        s_settled = sem("s_settled")
        s_zeroed = sem("s_zeroed")
        s_wattn = sem("s_wattn")
        s_wmix = sem("s_wmix")
        s_router = sem("s_router")
        s_b1 = sem("s_b1")
        s_w2 = sem("s_w2")
        s_decay = sem("s_decay")
        s_setup_pe = sem("s_setup_pe")
        s_setup_dve = sem("s_setup_dve")
        s_x_in = [[sem(f"s_x_in{l}{p}") for p in range(2)] for l in range(2)]

        NORM = "stats rstd xn xnp xT xTe x2T x2Te logits lgs st2 rs2 xn2 xn2p xnew "
        AS = {n: sem(f"a_{n}") for n in (NORM + "vkp qp relk relq v phik phi z zq kvT kv scores am upd "
                                         "state o oe y dmax rden").split()}
        BS = {n: sem(f"b_{n}") for n in (NORM + "scan mix sig vm").split()}
        s_rows = [[sem(f"s_rows{l}{p}") for p in range(2)] for l in range(2)]
        s_xrows = [sem(f"s_xrows{l}") for l in range(2)]
        s_route = [sem(f"s_route{l}") for l in range(2)]
        s_lexp = [sem(f"s_lexp{l}") for l in range(2)]
        s_oh = [sem(f"s_oh{l}") for l in range(2)]
        s_count = [sem(f"s_count{l}") for l in range(2)]
        s_etab = [sem(f"s_etab{l}") for l in range(2)]
        s_onehots = [sem(f"s_onehots{l}") for l in range(2)]
        s_pool1h = sem("s_pool1h")
        s_inv = [sem(f"s_inv{l}") for l in range(2)]
        s_idx = [sem(f"s_idx{l}") for l in range(2)]
        s_gates = [sem(f"s_gates{l}") for l in range(2)]
        s_gout = [sem(f"s_gout{l}") for l in range(2)]
        s_gat = [sem(f"s_gat{b}") for b in range(ND)]
        s_w1 = [sem(f"s_w1_{b}") for b in range(NW)]
        s_sct = [sem(f"s_sct{b}") for b in range(ND)]
        s_xsT = [sem(f"s_xsT{l}") for l in range(2)]
        s_xsTe = [sem(f"s_xsTe{l}") for l in range(2)]
        s_hA = [sem(f"s_hA{l}") for l in range(2)]
        s_hD = [sem(f"s_hD{l}") for l in range(2)]
        s_rA = [sem(f"s_rA{l}") for l in range(2)]
        s_rD = [sem(f"s_rD{l}") for l in range(2)]
        s_ye = [sem(f"s_ye{l}") for l in range(2)]
        s_pre = [sem(f"s_pre{l}") for l in range(2)]
        s_ys = [sem(f"s_ys{l}") for l in range(2)]

        def settle(eng, n):
            if not isinstance(n, int):
                eng.sem_inc(s_settled, 1)

        def tiles(g, n=GT):
            return bass.ds(g * GT, n)

        def slots(eng, slot):
            for k in range(3):
                slot(k // 2, k % 2)
            with eng.Fori(0, (NG - 4) // 2) as u:
                slot(u + 1, 1)
                slot(u + 2, 0)
            for k in range(NG - 1, NG + 2):
                slot(k // 2, k % 2)

        def live(m, p, back):
            q = (p - back) % 2
            mm = m + (p - back - q) // 2
            return None if isinstance(mm, int) and not 0 <= mm < NG // 2 else (mm, q)

        def slot_tiles(eng, step):
            for i in range(UN):
                step(i, i, 0)
            with eng.Fori(1, ST // UN) as u:
                for r in range(UN):
                    step(UN * u + r, r, u)
            for i in range(ST // UN * UN, ST):
                step(i, i % UN, i // UN)

        def ahead(i, r, n, by):
            if isinstance(i, int) and i + by >= ST:
                return None
            return i + by, (r + by) % UN, n + (r + by) // UN

        def dmas(l, b, n, nbuf=ND):
            return 16 * (l * len(range(b, ST, nbuf)) + n)

        LO_STEP = 18
        ONE_HOT_CUTS = (0, 9, 18, NT - 6)

        block = ctx.enter_context(nc.Block())

        @block.sync
        def _(sp):
            def load_x(l, m, p):
                after(sp, s_x_in[l][p], 16 * m)
                src = (xt, x_mid.rearrange("(n p) d -> p n d", p=P))[l]
                sp.dma_start(xres[:, tiles(2 * m + p), :], src[:, tiles(2 * m + p), :]).then_inc(s_x_in[l][p], 16)

            for l in range(2):
                S = (AS, BS)[l]
                load_x(l, 0, 0)
                load_x(l, 0, 1)
                if l == 0:
                    sp.dma_start(rtw[:], router_w).then_inc(s_router, 16)
                    sp.dma_start(rtb[:], router_b.rearrange("(o e) -> o e", o=1).to_broadcast([P, E])
                                 ).then_inc(s_router, 16)
                with sp.Fori(1, NG // 2) as m:
                    load_x(l, m, 0)
                    load_x(l, m, 1)
                if l == 0:
                    for dst, src in ((rwo, rw_o), (rwr, rw_r), (rwv, rw_v)):
                        sp.dma_start(dst[:], src).then_inc(s_wmix, 16)
                    for i, v in enumerate((time_decay, mix_v, mix_r)):
                        sp.dma_start(vec[:, i:i + 1], v.rearrange("(h o) -> h o", o=1)).then_inc(s_wmix, 16)
                    sp.dma_start(b1n[:], b1.rearrange("e (c f) -> (e c) f", c=C)).then_inc(s_b1, 16)
                    sp.dma_start(b2b[:].rearrange("p e d -> p (e d)"),
                                 b2.rearrange("e d -> (e d)").rearrange("(o n) -> o n", o=1).to_broadcast([P, E * D])
                                 ).then_inc(s_w2, 16)
                    for e in range(E):
                        sp.dma_start(w2s[:, e], w2[e].rearrange("(c f) d -> f c d", c=C)).then_inc(s_w2, 16)

                rows = rows_dram[l].rearrange("(n p) r -> p n r", p=P)

                def rows_out(m, p):
                    g = 2 * m + p
                    sp.wait_ge(S["xnew"], g + 1)
                    settle(sp, g)
                    sp.dma_start(rows[:, tiles(g), D:2 * D], xres[:, tiles(g), :]).then_inc(s_xrows[l], 16)
                    sp.wait_ge(S["xn2"], g + 1)
                    sp.wait_ge(S["xn2p"], g + 1)
                    settle(sp, g)
                    sp.dma_start(rows[:, tiles(g), 0:D], xn[1][p][:]).then_inc(s_rows[l][p], 16)

                with sp.Fori(0, NG // 2) as m:
                    rows_out(m, 0)
                    rows_out(m, 1)

                sp.wait_ge(s_gates[l], 2)
                sp.dma_start(rows[:, :, 2 * D:], gate[:]).then_inc(s_gout[l], 16)

                sp.wait_ge(s_etab[l], 1)

                def load_w1(i, r, n):
                    after(sp, s_hD[l], i - NW + 1)
                    e = sp.value_load(etab[0:1, bass.ds(i, 1)], min_val=0, max_val=E - 1)
                    sp.dma_start(w1s[r % NW][:], w1[bass.ds(e, 1)].rearrange("o d f -> (o d) f")
                                 ).then_inc(s_w1[r % NW], 16)

                slot_tiles(sp, load_w1)
                for b in range(ND):
                    sp.wait_ge(s_sct[b], dmas(l + 1, b, 0))

        @block.gpsimd
        def _(pool):
            nc.gpsimd.memset(ident[:], 0.0)
            nc.gpsimd.memset(causal[:], 1.0)
            nc.gpsimd.memset(before[:], 1.0)
            nc.gpsimd.memset(neg_half[:], -0.5)
            nc.gpsimd.memset(ones_col[:], 1.0)
            nc.gpsimd.memset(ones_bf[:], 1.0).then_inc(s_memset, 1)
            pool.wait_ge(s_memset, 1)
            nc.gpsimd.affine_select(out=ident[:], in_=ident[:], compare_op=ALU.not_equal, fill=1.0, base=0,
                                    pattern=[[-1, P]], channel_multiplier=1)
            nc.gpsimd.affine_select(out=causal[:], in_=causal[:], compare_op=ALU.is_ge, fill=0.0, base=0,
                                    pattern=[[1, P]], channel_multiplier=-1)
            nc.gpsimd.affine_select(out=before[:], in_=before[:], compare_op=ALU.is_gt, fill=0.0, base=0,
                                    pattern=[[1, P]], channel_multiplier=-1).then_inc(s_const, 1)

            def rstds(l, S, w, m, p):
                g = 2 * m + p
                moments, steps, used = (("stats", "rstd", "xn"), ("st2", "rs2", "xn2"))[w]
                pool.wait_ge(S[moments], 2 * g + 2)
                nc.gpsimd.tensor_scalar(nmean[:, w, p], mv[:, w, p, :, 0], -1.0, None, ALU.mult)
                nc.gpsimd.tensor_scalar(veps[:, w, p], mv[:, w, p, :, 1], EPS, None, ALU.add).then_inc(S[steps], 1)
                pool.wait_ge(S[steps], 3 * g + 1)
                after(pool, S[used], g - 1)
                nc.gpsimd.tensor_tensor(rstd[:, w, p], veps[:, w, p], neg_half[:], ALU.pow).then_inc(S[steps], 1)
                pool.wait_ge(S[steps], 3 * g + 2)
                after(pool, S[("xT", "x2T")[w]], g - 1)
                if w == 1:
                    after(pool, s_rows[l][p], 16 * m)
                nc.gpsimd.tensor_tensor(nmr[:, w, p], nmean[:, w, p], rstd[:, w, p], ALU.mult).then_inc(S[steps], 1)
                pool.wait_ge(S[steps], 3 * g + 3)

            def normalize(w, g, tiles_of_group):
                p = g % 2
                for j in tiles_of_group:
                    last = nc.gpsimd.tensor_scalar(xn[w][p][:, j], xres[:, g * GT + j], rstd[:, w, p, j:j + 1],
                                                   nmr[:, w, p, j:j + 1], ALU.mult, ALU.add)
                return last

            def norm1(l, S, m, p):
                g = 2 * m + p
                rstds(l, S, 0, m, p)
                normalize(0, g, range(NA[l], GT)).then_inc(S["xnp"], 1)

            def norm2(l, S, m, p):
                g = 2 * m + p
                rstds(l, S, 1, m, p)
                normalize(1, g, range(NA[l], GT)).then_inc(S["xn2p"], 1)

            def z_dot_q(k, p):
                pool.wait_ge(AS["z"], k + 1)
                pool.wait_ge(AS["phi"], k + 1)
                after(pool, AS["y"], k - 1)
                nc.gpsimd.tensor_tensor(op[p][0:H, :], zT[p][:], qT[p][:], ALU.mult).then_inc(AS["zq"], 1)

            for l in range(2):
                S = (AS, BS)[l]
                norm1(l, S, 0, 0)
                for k in range(NG + 2):
                    nxt, old = live(k // 2, k % 2, -1), live(k // 2, k % 2, 2)
                    if old:
                        norm2(l, S, *old)
                    if nxt:
                        norm1(l, S, *nxt)
                    if l == 0 and k < NG:
                        z_dot_q(k, k % 2)
                if l == 0:
                    nc.gpsimd.iota(rev8[:], pattern=[[-1, E]], base=E, channel_multiplier=0,
                                   allow_small_or_imprecise_dtypes=True)
                    nc.gpsimd.iota(iota_p[:], pattern=[[1, P]], base=0, channel_multiplier=0,
                                   allow_small_or_imprecise_dtypes=True)
                    nc.gpsimd.iota(iota_bf[:], pattern=[[1, P]], base=0, channel_multiplier=0,
                                   allow_small_or_imprecise_dtypes=True)
                    nc.gpsimd.iota(part1[:], pattern=[[0, 1]], base=1, channel_multiplier=1,
                                   allow_small_or_imprecise_dtypes=True)
                    nc.gpsimd.iota(tile_base[:], pattern=[[P, NT], [0, ST]], base=0, channel_multiplier=0,
                                   allow_small_or_imprecise_dtypes=True)
                    nc.gpsimd.iota(spare[:], pattern=[[P, ST]], base=TOK + 1, channel_multiplier=1,
                                   allow_small_or_imprecise_dtypes=True)
                    nc.gpsimd.memset(restart[:], 1.0).then_inc(s_memset, 1)
                    pool.wait_ge(s_memset, 2)
                    nc.gpsimd.memset(restart[:, :, 0:1], 0.0).then_inc(s_const, 1)

                pool.wait_ge(s_route[l], LO_STEP)
                for t in range(ONE_HOT_CUTS[-1], NT):
                    last = nc.gpsimd.tensor_scalar(lo1h[:, t], iota_p[:], lo[:, t:t + 1], None, ALU.is_equal)
                last.then_inc(s_pool1h, 1)

                for p in range(2):
                    pool.wait_ge(s_rows[l][p], 16 * (NG // 2))
                pool.wait_ge(s_xrows[l], 16 * NG)
                pool.wait_ge(s_gout[l], 16)
                pool.wait_ge(s_idx[l], 1)

                def gather(i):
                    after(pool, s_ys[l], i - ND + 1)
                    pool.indirect_dma_start(xs[i % ND][:], None, rows_dram[l],
                                            bass.IndirectOffsetOnAxis(ap=gidx[:, i:i + 1], axis=0)
                                            ).then_inc(s_gat[i % ND], 16)

                def scatter(i):
                    pool.wait_ge(s_ys[l], i + 1)
                    pool.indirect_dma_start(x_new[l], bass.IndirectOffsetOnAxis(ap=sidx[:, i:i + 1], axis=0),
                                            ys[i % ND][:], None, bounds_check=TOK - 1, oob_is_err=False
                                            ).then_inc(s_sct[i % ND], 16)

                for i in range(ND):
                    gather(i)
                pool.wait_ge(s_idx[l], 2)
                for i in range(ST):
                    scatter(i)
                    if i + ND < ST:
                        gather(i + ND)

        @block.scalar
        def _(act):
            act.dma_start(wvk[:, 0:H], w_v).then_inc(s_wattn, 16)
            act.dma_start(wvk[:, H:2 * H], w_k).then_inc(s_wattn, 16)
            act.dma_start(wq[:], w_q).then_inc(s_wattn, 16)
            act.wait_ge(s_zeroed, 1)
            act.dma_start(wox[H:P, 0:D], w_o).then_inc(s_wattn, 16)

            def evac_xT(S, m, p, dst, read):
                act.wait_ge(S["xT"], 2 * m + p + 1)
                after(act, *read)
                nc.scalar.copy(dst[:], bank[0][:]).then_inc(S["xTe"], 1)

            def evac_x2T(S, m, p):
                g = 2 * m + p
                act.wait_ge(S["x2T"], g + 1)
                after(act, S["logits"], g)
                nc.scalar.copy(xn2T[:], bank[X2_BANK[S is BS]][:]).then_inc(S["x2Te"], 1)

            def norm(l, w, m, p):
                S = (AS, BS)[l]
                g = 2 * m + p
                done, steps = (("xn", "rstd"), ("xn2", "rs2"))[w]
                act.wait_ge(S[steps], 3 * g + 3)
                settle(act, g)
                for j in range(NA[l]):
                    src = xres[:, bass.ds(g * GT + j, 1), :].rearrange("p o d -> p (o d)")
                    last = nc.scalar.activation(xn[w][p][:, j], src, ACT.Identity, bias=nmr[:, w, p, j:j + 1],
                                                scale=rstd[:, w, p, j:j + 1])
                last.then_inc(S[done], 1)

            def attn_slot(m, p):
                k = 2 * m + p
                if live(m, p, 0):
                    evac_xT(AS, m, p, xnT[0], (AS["qp"], k))
                    act.wait_ge(AS["vkp"], k + 1)
                    after(act, AS["phik"], k)
                    nc.scalar.activation(ex[H:P, :], bank[1][H:P, :], ACT.Exp)
                    nc.scalar.activation(rl[H:P, :], bank[1][H:P, :], ACT.Relu).then_inc(AS["relk"], 1)
                    after(act, AS["o"], k - 1)
                    nc.scalar.copy(vk[p][0:H, :], bank[1][0:H, :]).then_inc(AS["v"], 1)
                    act.wait_ge(AS["qp"], k + 1)
                    after(act, AS["phi"], k)
                    nc.scalar.activation(ex[0:H, :], bank[2][0:H, :], ACT.Exp)
                    nc.scalar.activation(rl[0:H, :], bank[2][0:H, :], ACT.Relu).then_inc(AS["relq"], 1)
                if live(m, p, 1):
                    q = live(m, p, 1)[1]
                    act.wait_ge(AS["o"], k)
                    after(act, AS["y"], k - 2)
                    nc.scalar.copy(op[q][H:P, :], bank[5][H:P, :]).then_inc(AS["oe"], 1)
                if live(m, p, 2):
                    norm(0, 1, *live(m, p, 2))
                if live(m, p, 0):
                    act.wait_ge(AS["kvT"], k + 1)
                    nc.scalar.copy(kv[p][:], bank[3][:].rearrange("p (j c) -> p j c", j=GT)).then_inc(AS["kv"], 1)
                if live(m, p, 2):
                    evac_x2T(AS, *live(m, p, 2))
                if live(m, p, -1):
                    norm(0, 0, *live(m, p, -1))

            def mix_slot(m, p):
                k = 2 * m + p
                if live(m, p, 0):
                    evac_xT(BS, m, p, xnT[p], (BS["mix"], k - 1))
                if live(m, p, -1):
                    norm(1, 0, *live(m, p, -1))
                if live(m, p, 2):
                    norm(1, 1, *live(m, p, 2))
                if live(m, p, 0):
                    act.wait_ge(BS["mix"], k + 1)
                    after(act, BS["vm"], k)
                    for i in range(2):
                        src = bank[(1, 4)[p] + i][:].rearrange("t (j w d) -> t j w d", j=2, w=2)[:, :, 1]
                        last = nc.scalar.activation(sg[:, 2 * i:2 * i + 2], src, ACT.Sigmoid)
                    last.then_inc(BS["sig"], 1)
                if live(m, p, 2):
                    evac_x2T(BS, *live(m, p, 2))

            def fetch_table(function):
                act.wait_ge(s_const, 1)
                nc.scalar.activation(unread[:], neg_half[:], function)

            for l in range(2):
                fetch_table((ACT.Exp, ACT.Sigmoid)[l])
                norm(l, 0, 0, 0)
                slots(act, (attn_slot, mix_slot)[l])
                if l == 1:
                    fetch_table(ACT.Exp)
                act.wait_ge(s_route[l], 2)
                nc.scalar.activation(le[:], ld[:], ACT.Exp).then_inc(s_lexp[l], 1)
                act.wait_ge(s_gates[l], 1)
                nc.scalar.copy(gate[:], gate1[:].unsqueeze(2).to_broadcast([P, NT, RW - 2 * D])
                               ).then_inc(s_gates[l], 1)

                act.wait_ge(s_etab[l], 1)
                if l == 0:
                    act.wait_ge(s_wmix, 16 * 6)
                    nc.scalar.activation(edec[:], vec[:, 0:1], ACT.Exp).then_inc(s_decay, 1)
                    act.wait_ge(s_decay, 1)
                    nc.scalar.activation(decay[:], edec[:], ACT.Exp, scale=-1.0).then_inc(s_decay, 1)
                    act.wait_ge(s_setup_dve, 2)

                def evac_xs(i, r, n):
                    act.wait_ge(s_xsT[l], i + 1)
                    after(act, s_hD[l], i - NB + 1)
                    nc.scalar.copy(xsT[r % NB][:], bank[r % 2][:, 0:P]).then_inc(s_xsTe[l], 1)

                def relu(i, r, n):
                    e = act.value_load(etab[0:1, bass.ds(i, 1)], min_val=0, max_val=E - 1)
                    act.wait_ge(s_hA[l], i + 1)
                    after(act, s_ye[l], i - NB + 1)
                    for c in range(C // 2):
                        last = nc.scalar.activation(hT[r % NB][:, c], bank[2 + r % 2][:, c * P:(c + 1) * P], ACT.Relu,
                                                    bias=b1T[:, bass.ds(e * C + c, 1)])
                    last.then_inc(s_rA[l], 1)

                def step(*at):
                    if ahead(*at, 2):
                        evac_xs(*ahead(*at, 2))
                    if ahead(*at, 1):
                        relu(*ahead(*at, 1))

                evac_xs(0, 0, 0)
                evac_xs(1, 1, 0)
                relu(0, 0, 0)
                slot_tiles(act, step)

        @block.vector
        def _(dve):
            def tile_of(g, j):
                return xres[:, bass.ds(g * GT + j, 1), :].rearrange("p o d -> p (o d)")

            def stats_of(S, w, m, p):
                g = 2 * m + p
                after(dve, S[("stats", "st2")[w]], 2 * g)
                settle(dve, g)
                for j in range(GT):
                    last = nc.vector.bn_stats(stats[:, w, j], tile_of(g, j))
                last.then_inc(S[("stats", "st2")[w]], 1)

            def moments(S, w, m, p):
                g = 2 * m + p
                dve.wait_ge(S[("stats", "st2")[w]], 2 * g + 1)
                for n in (("xn", "xnp"), ("xn2", "xn2p"))[w]:
                    after(dve, S[n], g - 1)
                settle(dve, g)
                for j in range(GT):
                    last = nc.vector.bn_aggr(mv[:, w, p, j], stats[:, w, j])
                last.then_inc(S[("stats", "st2")[w]], 1)

            def first_stats(l, m, p):
                dve.wait_ge(s_x_in[l][p], 16 * (m + 1))
                stats_of((AS, BS)[l], 0, m, p)

            def logits_out(S, m, p):
                g = 2 * m + p
                dve.wait_ge(S["logits"], g + 1)
                nc.vector.tensor_tensor(lg[:, tiles(g), :],
                                        bank[LG_BANK[S is BS]][:, 0:GT * E].rearrange("p (j e) -> p j e", j=GT),
                                        rtb[:].unsqueeze(1).to_broadcast([P, GT, E]), ALU.add).then_inc(S["lgs"], 1)

            def attn_slot(m, p):
                k = 2 * m + p
                back = live(m, p, 1)
                if back:
                    mm, q = back
                    dve.wait_ge(AS["scores"], k)
                    after(dve, AS["o"], k - 1)
                    nc.vector.tensor_tensor(am[:], bank[4][:].rearrange("p (j t) -> p j t", j=GT),
                                            causal[:].unsqueeze(1).to_broadcast([P, GT, P]), ALU.mult
                                            ).then_inc(AS["am"], 1)
                    dve.wait_ge(AS["upd"], k)
                    n = GT if q == 0 else GT - 1
                    upd = bank[5][0:H, 0:H * n].rearrange("v (j k) -> v j k", j=n)
                    if q == 0:
                        nc.vector.tensor_copy(state[0][:], upd).then_inc(AS["state"], 1)
                    else:
                        dve.wait_ge(AS["state"], k - 1)
                        nc.vector.tensor_tensor(state[1][:, 0:n], upd,
                                                state[0][:, GT - 1:GT].to_broadcast([H, n, H]), ALU.add
                                                ).then_inc(AS["state"], 1)
                nxt = live(m, p, -1)
                if nxt:
                    first_stats(0, *nxt)
                if live(m, p, 0):
                    dve.wait_ge(AS["relk"], k + 1)
                    nc.vector.scalar_tensor_tensor(out=vk[p][H:P, :], in0=ex[H:P, :], scalar=1.0, in1=rl[H:P, :],
                                                   op0=ALU.min, op1=ALU.add).then_inc(AS["phik"], 1)
                if nxt:
                    moments(AS, 0, *nxt)
                if live(m, p, 0):
                    dve.wait_ge(AS["relq"], k + 1)
                    after(dve, AS["zq"], k - 1)
                    nc.vector.scalar_tensor_tensor(out=qT[p][:], in0=ex[0:H, :], scalar=1.0, in1=rl[0:H, :],
                                                   op0=ALU.min, op1=ALU.add).then_inc(AS["phi"], 1)
                    dve.wait_ge(AS["phik"], k + 1)
                    after(dve, AS["z"], k)
                    nc.vector.tensor_tensor_scan(zT[p][:], ones_col[H:P, 0:1].to_broadcast([H, GW]), vk[p][H:P, :],
                                                 0.0 if p == 0 else zT[0][:, GW - 1:GW], ALU.mult, ALU.add
                                                 ).then_inc(AS["z"], 1)
                if back:
                    dve.wait_ge(AS["y"], k)
                    outs = [bank[6 + i][:, 0:2 * YC].rearrange("p (j c) -> p j c", j=2) for i in range(2)]
                    for i in range(2):
                        last = nc.vector.tensor_scalar(rden[:, 0, 2 * i:2 * i + 2], outs[i][:, :, D], 1e-6, None,
                                                       ALU.max)
                    last.then_inc(AS["dmax"], 1)
                    dve.wait_ge(AS["dmax"], k)
                    nc.vector.reciprocal(rden[:, 1], rden[:, 0]).then_inc(AS["rden"], 1)
                    dve.wait_ge(AS["rden"], k)
                    for j in range(GT):
                        t = tile_of(k - 1, j)
                        last = nc.vector.scalar_tensor_tensor(out=t, in0=outs[j // 2][:, j % 2, 0:D],
                                                              scalar=rden[:, 1, j:j + 1], in1=t,
                                                              op0=ALU.mult, op1=ALU.add)
                    last.then_inc(AS["xnew"], 1)
                    dve.wait_ge(AS["xnew"], k)
                    stats_of(AS, 1, mm, q)
                if back:
                    moments(AS, 1, mm, q)
                if live(m, p, 2):
                    logits_out(AS, *live(m, p, 2))

            def mix_slot(m, p):
                k = 2 * m + p
                back = live(m, p, 1)
                if live(m, p, -1):
                    first_stats(1, *live(m, p, -1))
                if back:
                    mm, q = back
                    dve.wait_ge(BS["sig"], k)
                    after(dve, BS["xnew"], k - 1)
                    for i in range(2):
                        val = bank[(1, 4)[q] + i][:].rearrange("t (j w d) -> t j w d", j=2, w=2)[:, :, 0]
                        last = nc.vector.tensor_tensor(tm[:, 2 * i:2 * i + 2], sg[:, 2 * i:2 * i + 2], val, ALU.mult)
                    last.then_inc(BS["vm"], 1)
                if live(m, p, -1):
                    moments(BS, 0, *live(m, p, -1))
                if live(m, p, 0):
                    dve.wait_ge(BS["xTe"], k + 1)
                    after(dve, BS["mix"], k - 1)
                    after(dve, BS["scan"], k)
                    if p == 1:
                        nc.vector.tensor_copy(sc[1][:, 0:1], sc[0][:, GW:GW + 1])
                    nc.vector.tensor_tensor_scan(sc[p][:, 1:1 + GW], decay[:, 0:1].to_broadcast([P, GW]), xnT[p][:],
                                                 0.0 if p == 0 else sc[0][:, GW:GW + 1], ALU.mult, ALU.add
                                                 ).then_inc(BS["scan"], 1)
                if back:
                    dve.wait_ge(BS["vm"], k)
                    nc.vector.tensor_tensor(xres[:, tiles(k - 1), :], xres[:, tiles(k - 1), :], tm[:], ALU.add
                                            ).then_inc(BS["xnew"], 1)
                if back:
                    dve.wait_ge(BS["xnew"], k)
                    stats_of(BS, 1, mm, q)
                if live(m, p, 3):
                    logits_out(BS, *live(m, p, 3))
                if back:
                    moments(BS, 1, mm, q)

            def route(l):
                n = [0]

                def step(ins):
                    n[0] += 1
                    ins.then_inc(s_route[l], 1)
                    dve.wait_ge(s_route[l], n[0])

                def per_tile(a, k=E):
                    return a.unsqueeze(2).to_broadcast([P, NT, k])

                dve.wait_ge((AS, BS)[l]["lgs"], NG + 1)
                dve.wait_ge(s_const, 2)
                step(nc.vector.tensor_reduce(mx[:], lg[:], AX_X, ALU.max))
                step(nc.vector.tensor_tensor(ld[:], lg[:], per_tile(mx[:]), ALU.subtract))
                step(nc.vector.scalar_tensor_tensor(out=rv[:], in0=ld[:], scalar=0.0,
                                                    in1=rev8[:].unsqueeze(1).to_broadcast([P, NT, E]),
                                                    op0=ALU.is_equal, op1=ALU.mult))
                step(nc.vector.tensor_reduce(top[:], rv[:], AX_X, ALU.max))
                nc.vector.tensor_tensor(oh[:], rev8[:].unsqueeze(1).to_broadcast([P, NT, E]), per_tile(top[:]),
                                        ALU.is_equal).then_inc(s_oh[l], 1)
                dve.wait_ge(s_lexp[l], 1)
                step(nc.vector.tensor_reduce(sm[:], le[:], AX_X, ALU.add))
                nc.vector.reciprocal(gate1[:], sm[:]).then_inc(s_gates[l], 1)
                dve.wait_ge(s_count[l], 1)
                step(nc.vector.tensor_copy(tot[:], bank[2][:, 0:NT * E].rearrange("p (t e) -> p e t", e=E)))
                step(nc.vector.tensor_tensor_scan(cum[:].rearrange("p e t -> p (e t)"),
                                                  restart[:].rearrange("p e t -> p (e t)"),
                                                  tot[:].rearrange("p e t -> p (e t)"), 0.0, ALU.mult, ALU.add))
                nc.vector.tensor_tensor(exc[:], cum[:], tot[:], ALU.subtract)
                step(nc.vector.tensor_scalar(etiles[:, 0], cum[:, :, NT - 1], 1.0 / P, (P - 1) / 2 / P, ALU.mult, ALU.add))
                step(nc.vector.tensor_scalar(etiles[:, 1], etiles[:, 0], ROUND, -ROUND, ALU.add, ALU.add))
                step(nc.vector.tensor_tensor_scan(etiles[:, 2], ones_col[:, 0:1].to_broadcast([P, E]), etiles[:, 1],
                                                  0.0, ALU.mult, ALU.add))
                step(nc.vector.tensor_tensor(ebase[:], etiles[:, 2], etiles[:, 1], ALU.subtract))
                step(nc.vector.scalar_tensor_tensor(out=slot_e[:], in0=ebase[:].unsqueeze(2).to_broadcast([P, E, NT]),
                                                    scalar=float(P), in1=exc[:], op0=ALU.mult, op1=ALU.add))
                step(nc.vector.tensor_tensor(tot[:], bank[1][:, 0:NT * E].rearrange("p (t e) -> p e t", e=E), slot_e[:],
                                             ALU.add))
                step(nc.vector.tensor_tensor(cum[:], tot[:], oh[:].rearrange("p t e -> p e t"), ALU.mult))
                step(nc.vector.tensor_reduce(pos[:], cum[:].rearrange("p e t -> p t e"), AX_X, ALU.add))
                step(nc.vector.tensor_scalar(hi[:], pos[:], 1.0 / P, -(P - 1) / 2 / P, ALU.mult, ALU.add))
                step(nc.vector.tensor_scalar(hi_bf[:], hi[:], ROUND, -ROUND, ALU.add, ALU.add))
                step(nc.vector.scalar_tensor_tensor(out=lo[:], in0=hi_bf[:], scalar=-float(P), in1=pos[:],
                                                    op0=ALU.mult, op1=ALU.add))
                step(nc.vector.tensor_tensor(hi1h[:], iota_bf[:, 0:ST].unsqueeze(1).to_broadcast([P, NT, ST]),
                                             per_tile(hi_bf[:], ST), ALU.is_equal))
                nc.vector.tensor_scalar(hid[:, :, 0], hi1h[:], part1[:, 0:1], None, ALU.mult)
                nc.vector.tensor_tensor(hid[:, :, 1], hi1h[:], tile_base[:], ALU.mult).then_inc(s_onehots[l], 1)
                for t0, t1 in zip(ONE_HOT_CUTS, ONE_HOT_CUTS[1:]):
                    nc.vector.tensor_tensor(lo1h[:, t0:t1], iota_p[:].unsqueeze(1).to_broadcast([P, t1 - t0, P]),
                                            lo[:, t0:t1].unsqueeze(2).to_broadcast([P, t1 - t0, P]), ALU.is_equal
                                            ).then_inc(s_onehots[l], 1)
                step(nc.vector.tensor_tensor(ecmp[:], iota_p[0:1, 0:ST].unsqueeze(2).to_broadcast([1, ST, E]),
                                             etiles[0:1, 2].unsqueeze(1).to_broadcast([1, ST, E]), ALU.is_ge))
                step(nc.vector.tensor_reduce(ecnt[:], ecmp[:], AX_X, ALU.add))
                nc.vector.tensor_scalar(etab[0:1, 0:ST], ecnt[:], float(E - 1), None, ALU.min).then_inc(s_etab[l], 1)
                dve.wait_ge(s_inv[l], 1)
                step(nc.vector.tensor_copy(ivh[:], bank[4][:, 0:ST]))
                step(nc.vector.tensor_tensor(iv[:], bank[4][:, ST:2 * ST], ivh[:], ALU.add))
                nc.vector.tensor_scalar(gidx[:], iv[:], -1.0, 0.0, ALU.add, ALU.max).then_inc(s_idx[l], 1)
                step(nc.vector.scalar_tensor_tensor(out=ivz[:], in0=iv[:], scalar=0.0, in1=spare[:],
                                                    op0=ALU.is_equal, op1=ALU.mult))
                nc.vector.scalar_tensor_tensor(out=sidx[:], in0=iv[:], scalar=-1.0, in1=ivz[:],
                                               op0=ALU.add, op1=ALU.add).then_inc(s_idx[l], 1)

            def mix_weights():
                dve.wait_ge(s_setup_pe, 1)
                nc.vector.tensor_copy(rwoT[:], bank[7][:, 0:P]).then_inc(s_setup_dve, 1)
                nc.vector.tensor_copy(b1T[:], bank[7][:, 2 * P:2 * P + E * C])
                nc.vector.tensor_scalar(mix_c[:], vec[:, 1:3], -1.0, 1.0, ALU.mult, ALU.add).then_inc(s_setup_dve, 1)
                dve.wait_ge(s_setup_pe, 2)
                dve.wait_ge(s_setup_dve, 2)
                for w in range(2):
                    src = (bank[6][:, 0:P], bank[7][:, P:2 * P])[w]
                    nc.vector.tensor_scalar(wx[:, w], src, vec[:, 1 + w:2 + w], None, ALU.mult)
                    last = nc.vector.tensor_scalar(wp[:, w], src, mix_c[:, w:w + 1], None, ALU.mult)
                last.then_inc(s_setup_dve, 1)

            def experts(l):
                def hidden(i, r, n):
                    e = dve.value_load(etab[0:1, bass.ds(i, 1)], min_val=0, max_val=E - 1)
                    dve.wait_ge(s_gat[r], dmas(l, r, n + 1))
                    nc.vector.scalar_tensor_tensor(out=xs[r % ND][:, D:2 * D],
                                                   in0=b2b[:, bass.ds(e, 1), :].rearrange("p o d -> p (o d)"),
                                                   scalar=xs[r % ND][:, 2 * D:2 * D + 1], in1=xs[r % ND][:, D:2 * D],
                                                   op0=ALU.mult, op1=ALU.add).then_inc(s_pre[l], 1)
                    dve.wait_ge(s_hD[l], i + 1)
                    after(dve, s_ye[l], i - NB + 1)
                    for c in range(C // 2, C):
                        f = (c - C // 2) * P
                        last = nc.vector.tensor_scalar(hT[r % NB][:, c], bank[4 + r % 2][:, f:f + P],
                                                       b1T[:, bass.ds(e * C + c, 1)], 0.0, ALU.add, ALU.max)
                    last.then_inc(s_rD[l], 1)

                def add_y(i, r, n):
                    b = r % ND
                    dve.wait_ge(s_ye[l], i + 1)
                    dve.wait_ge(s_pre[l], i + 1)
                    after(dve, s_sct[b], dmas(l, b, n))
                    nc.vector.scalar_tensor_tensor(out=ys[b][:], in0=bank[6 + r % 2][:, 0:P],
                                                   scalar=xs[b][:, 2 * D:2 * D + 1], in1=xs[b][:, D:2 * D],
                                                   op0=ALU.mult, op1=ALU.add).then_inc(s_ys[l], 1)

                def step(*at):
                    if ahead(*at, 1):
                        hidden(*ahead(*at, 1))
                    add_y(*at)

                dve.wait_ge(s_etab[l], 1)
                if l == 0:
                    mix_weights()
                dve.wait_ge(s_w2, 16 * (1 + E))
                hidden(0, 0, 0)
                slot_tiles(dve, step)

            for S in (AS, BS):
                dve.sem_inc(S["lgs"], 1)
            nc.vector.memset(wox[:], 0.0).then_inc(s_zeroed, 1)
            dve.wait_ge(s_zeroed, 1)
            nc.vector.memset(wox[0:H, D:YC], 1.0).then_inc(s_zeroed, 1)
            nc.vector.memset(sc[0][:, 0:1], 0.0)
            first_stats(0, 0, 0)
            moments(AS, 0, 0, 0)

            slots(dve, attn_slot)
            route(0)
            experts(0)
            first_stats(1, 0, 0)
            moments(BS, 0, 0, 0)
            slots(dve, mix_slot)
            logits_out(BS, NG // 2 - 1, 1)
            route(1)
            experts(1)

        @block.tensor
        def _(pe):
            def transpose_x(S, m, p):
                g = 2 * m + p
                pe.wait_ge(S["xn"], g + 1)
                pe.wait_ge(S["xnp"], g + 1)
                if S is AS:
                    after(pe, S["x2Te"], g - 2)
                else:
                    after(pe, S["xTe"], g)
                for j in range(GT):
                    last = nc.tensor.transpose(bank[0][:, j * P:(j + 1) * P], xn[0][p][:, j], ident[:])
                last.then_inc(S["xT"], 1)

            def transpose_x2(S, m, p):
                g = 2 * m + p
                pe.wait_ge(S["xn2"], g + 1)
                pe.wait_ge(S["xn2p"], g + 1)
                if S is AS:
                    pe.wait_ge(S["xTe"], min(g + 3, NG) if isinstance(g, int) else g + 3)
                else:
                    after(pe, S["x2Te"], g)
                for j in range(GT):
                    last = nc.tensor.transpose(bank[X2_BANK[S is BS]][:, j * P:(j + 1) * P], xn[1][p][:, j], ident[:])
                last.then_inc(S["x2T"], 1)

            def logits(S, m, p):
                g = 2 * m + p
                pe.wait_ge(S["x2Te"], g + 1)
                pe.wait_ge(S["lgs"], g + 1)
                if S is AS:
                    pe.wait_ge(S["kv"], min(g + 3, NG) if isinstance(g, int) else g + 3)
                for j in range(GT):
                    last = nc.tensor.matmul(bank[LG_BANK[S is BS]][:, E * j:E * (j + 1)], xn2T[:, j * P:(j + 1) * P],
                                            rtw[:], start=True, stop=True)
                last.then_inc(S["logits"], 1)

            def attn_slot(m, p):
                k = 2 * m + p
                cur, back, old = live(m, p, 0), live(m, p, 1), live(m, p, 2)
                if cur:
                    transpose_x(AS, m, p)
                if back:
                    mm, q = back
                    pe.wait_ge(AS["phi"], k)
                    after(pe, AS["am"], k - 1)
                    for j in range(GT):
                        t = slice(j * P, (j + 1) * P)
                        last = nc.tensor.matmul(bank[4][:, t], vk[q][0:H, t], qT[q][:, t], start=True, stop=True)
                    last.then_inc(AS["scores"], 1)
                if cur:
                    pe.wait_ge(AS["xTe"], k + 1)
                    after(pe, AS["relq"], k)
                    after(pe, AS["v"], k)
                    nc.tensor.matmul(bank[1][:], wvk[:], xnT[0][:], start=True, stop=True).then_inc(AS["vkp"], 1)
                if back:
                    pe.wait_ge(AS["kv"], k)
                    after(pe, AS["state"], k - 1)
                    settle(pe, k)
                    n = GT if q == 0 else GT - 1
                    for j in range(n):
                        last = nc.tensor.matmul(bank[5][0:H, H * j:H * n].rearrange("v (i k) -> v i k", k=H),
                                                kv[q][:, j, 0:H],
                                                kv[q][:, j:j + 1, H:2 * H].to_broadcast([P, n - j, H]),
                                                start=(j == 0), stop=(j == n - 1))
                    last.then_inc(AS["upd"], 1)
                if cur:
                    nc.tensor.matmul(bank[2][0:H, :], wq[:], xnT[0][:], start=True, stop=True).then_inc(AS["qp"], 1)
                if back:
                    pe.wait_ge(AS["am"], k)
                    pe.wait_ge(AS["state"], k)
                    after(pe, AS["oe"], k - 1)
                    settle(pe, k)
                    for j in range(GT):
                        t = slice(j * P, (j + 1) * P)
                        first = q == 0 and j == 0
                        last = nc.tensor.matmul(bank[5][H:P, t], kv[q][:, j, H:2 * H], am[:, j], start=True, stop=first)
                        if not first:
                            before_t = state[q][:, j - 1] if j > 0 else state[0][:, GT - 1]
                            last = nc.tensor.matmul(bank[5][H:P, t], before_t, qT[q][:, t], start=False, stop=True)
                    last.then_inc(AS["o"], 1)
                if cur:
                    pe.wait_ge(AS["phik"], k + 1)
                    pe.wait_ge(AS["v"], k + 1)
                    after(pe, AS["kv"], k)
                    after(pe, AS["lgs"], k - 1)
                    for j in range(GT):
                        last = nc.tensor.transpose(bank[3][:, j * P:(j + 1) * P], vk[p][:, j * P:(j + 1) * P],
                                                   ident[:])
                    last.then_inc(AS["kvT"], 1)
                if back:
                    pe.wait_ge(AS["oe"], k)
                    pe.wait_ge(AS["zq"], k)
                    for j in range(GT):
                        last = nc.tensor.matmul(bank[6 + j // 2][:, YC * (j % 2):YC * (j % 2 + 1)],
                                                op[q][:, j * P:(j + 1) * P], wox[:], start=True, stop=True)
                    last.then_inc(AS["y"], 1)
                if old:
                    transpose_x2(AS, *old)
                    logits(AS, *old)

            def mix_slot(m, p):
                k = 2 * m + p
                cur, old = live(m, p, 0), live(m, p, 2)
                if cur:
                    transpose_x(BS, m, p)
                if live(m, p, 3):
                    logits(BS, *live(m, p, 3))
                if cur:
                    pe.wait_ge(BS["scan"], k + 1)
                    pe.wait_ge(BS["xTe"], k + 1)
                    after(pe, BS["vm"], k - 1)
                    for j in range(GT):
                        t = slice(j * P, (j + 1) * P)
                        o = bank[(1, 4)[p] + j // 2][:, 2 * P * (j % 2):2 * P * (j % 2 + 1)]
                        nc.tensor.matmul(o, xnT[p][:, t], wx[:].rearrange("p w d -> p (w d)"), start=True, stop=False)
                        last = nc.tensor.matmul(o, sc[p][:, t], wp[:].rearrange("p w d -> p (w d)"),
                                                start=False, stop=True)
                    last.then_inc(BS["mix"], 1)
                if old:
                    transpose_x2(BS, *old)

            def setup_transposes():
                pe.wait_ge(s_wmix, 16 * 6)
                pe.wait_ge(s_b1, 16)
                pe.wait_ge(AS["xnew"], NG)
                nc.tensor.transpose(bank[7][:, 0:P], rwo[:], ident[:])
                nc.tensor.transpose(bank[7][:, P:2 * P], rwr[:], ident[:])
                nc.tensor.transpose(bank[7][:, 2 * P:2 * P + E * C], b1n[:], ident[0:E * C, 0:E * C]
                                    ).then_inc(s_setup_pe, 1)

            def setup_product():
                pe.wait_ge(s_setup_dve, 1)
                nc.tensor.matmul(bank[6][:, 0:P], rwv[:], rwoT[:], start=True, stop=True).then_inc(s_setup_pe, 1)

            def route(l):
                pe.wait_ge(s_oh[l], 1)
                ohf = oh[:].rearrange("p t e -> p (t e)")
                nc.tensor.matmul(bank[1][:, 0:NT * E], before[:], ohf, start=True, stop=True)
                nc.tensor.matmul(bank[2][:, 0:NT * E], ones_bf[:], ohf, start=True, stop=True).then_inc(s_count[l], 1)
                for t in range(NT):
                    if t in ONE_HOT_CUTS[:-1]:
                        pe.wait_ge(s_onehots[l], 2 + ONE_HOT_CUTS.index(t))
                    if t == ONE_HOT_CUTS[-1]:
                        pe.wait_ge(s_pool1h, l + 1)
                    last = nc.tensor.matmul(bank[4][:, 0:2 * ST], lo1h[:, t], hid[:, t].rearrange("p w s -> p (w s)"),
                                            start=(t == 0), stop=(t == NT - 1))
                last.then_inc(s_inv[l], 1)

            def experts(l):
                def turn(i, r, n):
                    pe.wait_ge(s_gat[r], dmas(l, r, n + 1))
                    after(pe, s_xsTe[l], i - 1)
                    nc.tensor.transpose(bank[r % 2][:, 0:P], xs[r % ND][:, 0:D], ident[:]).then_inc(s_xsT[l], 1)

                def first(i, r, n):
                    pe.wait_ge(s_xsTe[l], i + 1)
                    pe.wait_ge(s_w1[r % NW], dmas(l, r % NW, UN // NW * n + r // NW + 1, NW))
                    for half, ready, used in ((0, s_hA[l], s_rA[l]), (1, s_hD[l], s_rD[l])):
                        after(pe, used, i - 1)
                        for c in range(C // 2):
                            f = (half * (C // 2) + c) * P
                            mm = nc.tensor.matmul(bank[2 + 2 * half + r % 2][:, c * P:(c + 1) * P],
                                                  w1s[r % NW][:, f:f + P], xsT[r % NB][:], start=True, stop=True)
                        mm.then_inc(ready, 1)

                def second(i, r, n):
                    e = pe.value_load(etab[0:1, bass.ds(i, 1)], min_val=0, max_val=E - 1)
                    pe.wait_ge(s_rA[l], i + 1)
                    pe.wait_ge(s_rD[l], i + 1)
                    after(pe, s_ys[l], i - 1)
                    for c in range(C):
                        mm = nc.tensor.matmul(bank[6 + r % 2][:, 0:P], hT[r % NB][:, c],
                                              w2s[:, bass.ds(e, 1), c, :].rearrange("p o d -> p (o d)"),
                                              start=(c == 0), stop=(c == C - 1))
                    mm.then_inc(s_ye[l], 1)

                def step(*at):
                    if ahead(*at, 2):
                        turn(*ahead(*at, 2))
                    if ahead(*at, 1):
                        first(*ahead(*at, 1))
                    second(*at)

                pe.wait_ge(s_etab[l], 1)
                if l == 0:
                    setup_product()
                    pe.wait_ge(s_setup_dve, 3)
                    pe.wait_ge(s_w2, 16 * (1 + E))
                turn(0, 0, 0)
                turn(1, 1, 0)
                first(0, 0, 0)
                slot_tiles(pe, step)

            pe.wait_ge(s_const, 1)
            pe.wait_ge(s_wattn, 64)
            pe.wait_ge(s_zeroed, 2)
            pe.wait_ge(s_router, 32)

            slots(pe, attn_slot)
            setup_transposes()
            route(0)
            experts(0)
            slots(pe, mix_slot)
            logits(BS, NG // 2 - 1, 1)
            route(1)
            experts(1)


_INS = ['L0_attn_a_x', 'L0_attn_a_W_q', 'L0_attn_a_W_k', 'L0_attn_a_W_v', 'L0_attn_a_W_o',
        'L0_attn_b_time_decay', 'L0_attn_b_time_mix_v', 'L0_attn_b_time_mix_r',
        'L0_attn_b_Wv', 'L0_attn_b_Wr', 'L0_attn_b_Wo',
        'L0_ffn_router_W', 'L0_ffn_router_b', 'L0_ffn_W1', 'L0_ffn_b1', 'L0_ffn_W2', 'L0_ffn_b2']


def kernel(**inputs):
    import numpy as _np
    import concourse.bacc as _bacc
    from concourse import mybir as _mybir
    from concourse.bass_utils import run_bass_kernel_spmd as _run

    nc = _bacc.Bacc("TRN2", target_bir_lowering=False, num_devices=1)
    arrays, args = {}, []
    for name in _INS:
        a = _np.ascontiguousarray(inputs[name])
        arrays[f"in_{name}"] = a
        args.append(nc.dram_tensor(f"in_{name}", a.shape, _mybir.dt.from_np(a.dtype), kind="ExternalInput").ap())
    out = nc.dram_tensor("out", inputs['L0_attn_a_x'].shape, _mybir.dt.float32, kind="ExternalOutput").ap()
    hybrid_block(nc, *args, out)
    r = _run(nc, [arrays], core_ids=[0])
    return r.results[0]["out"]
```
